# Optimizing a Trainium2 kernel written in Bass

```python
import numpy as np
import jax
import jax.numpy as jnp

def _softmax(x, axis=-1):
    return jax.nn.softmax(x, axis=axis)

def _gelu(x):
    return jax.nn.gelu(x, approximate=True)

def _silu(x):
    return jax.nn.silu(x)

def _sigmoid(x):
    return jax.nn.sigmoid(x)

def _layernorm(x, axis=-1, eps=1e-05):
    m = jnp.mean(x, axis=axis, keepdims=True)
    v = jnp.var(x, axis=axis, keepdims=True)
    return (x - m) / jnp.sqrt(v + eps)

def _scatter_add(tgt, idx, src, axis=0):
    return tgt.at[idx].add(src)

def _segment_sum(src, seg, n):
    return jax.ops.segment_sum(src, seg, n)
kernel_name = 'mk_xattn_ffn_d1_seqx_r4_38ef25'

def setup_inputs(seed: int=0):
    np.random.seed(seed)
    _w = jnp.asarray

    def _rec_inputs():
        import jax
        import jax.numpy as jnp
        _rk = jax.random.key(seed)
        x = -0.0003929 + 0.9999 * jax.random.normal(jax.random.fold_in(_rk, 1), (128, 128, 256), jnp.float32)
        _lenS = 128 - jax.random.randint(jax.random.fold_in(_rk, 7), (128,), 0, max(1, 128 // 4) + 1, jnp.int32)
        _lenS2 = 128 - jax.random.randint(jax.random.fold_in(_rk, 8), (128,), 0, max(1, 128 // 4) + 1, jnp.int32)
        _ctx_1024P = jax.random.normal(jax.random.fold_in(_rk, 11), (128, 16, 256), jnp.float32)
        _ctx_1024c = jax.random.dirichlet(jax.random.fold_in(_rk, 511), 0.3 * jnp.ones((16,), jnp.float32), (128, 128))
        _ctx_1024t = jnp.einsum('bsk,bkd->bsd', _ctx_1024c, _ctx_1024P)
        _ctx_1024t = _ctx_1024t * jax.lax.rsqrt(jnp.mean(jnp.square(_ctx_1024t)) + 1e-12) * 0.953939
        ctx_1024 = 2.81802e-05 + 1.00001 * (_ctx_1024t + 0.3 * jax.random.normal(jax.random.fold_in(_rk, 611), (128, 128, 256), jnp.float32))
        itok_BxSx2_0_63 = jax.random.randint(jax.random.fold_in(_rk, 12), (128, 128, 2), 0, 64, jnp.int32)
        return (x, ctx_1024, itok_BxSx2_0_63)
    x, ctx_1024, itok_BxSx2_0_63 = _rec_inputs()

    def _L0_xattn_setup():
        import jax, jax.numpy as jnp
        import numpy as np
        DIM = 256
        NUM_HEADS = 16
        HEAD_DIM = DIM // NUM_HEADS
        SCALE = HEAD_DIM ** (-0.5)
        key = jax.random.key(seed)
        ks = jax.random.split(key, 10)
        B, N, C = (8, 512, DIM)
        std = C ** (-0.5)
        return {'query': jax.random.normal(ks[0], (B, N, C), jnp.float32), 'key': jax.random.normal(ks[1], (B, N, C), jnp.float32), 'value': jax.random.normal(ks[2], (B, N, C), jnp.float32), 'xpos': jax.random.randint(ks[3], (B, N, 2), 0, 64), 'ypos': jax.random.randint(ks[4], (B, N, 2), 0, 64), 'Wq': jax.random.normal(ks[5], (C, C), jnp.float32) * std, 'Wk': jax.random.normal(ks[6], (C, C), jnp.float32) * std, 'Wv': jax.random.normal(ks[7], (C, C), jnp.float32) * std, 'Wp': jax.random.normal(ks[8], (C, C), jnp.float32) * std, 'bp': jax.random.normal(ks[9], (C,), jnp.float32) * std}
    _L0_xattn_all = _L0_xattn_setup()
    _L0_xattn_in = {k: v for k, v in _L0_xattn_all.items() if k in ('Wq', 'Wk', 'Wv', 'Wp', 'bp')}
    del _L0_xattn_all

    def _L0_ffn_setup():
        import jax, jax.numpy as jnp
        import numpy as np
        TOP_K = 2
        key = jax.random.key(seed)
        ks = jax.random.split(key, 7)
        B, L, D, H, E, S = (2, 512, 256, 128, 16, 512)
        s = lambda fan_in: (1.0 / np.sqrt(fan_in)).astype(np.float32)
        return {'x': jax.random.normal(ks[0], (B, L, D), jnp.float32), 'gate_w': jax.random.normal(ks[1], (E, D), jnp.float32) * s(D), 'w1': jax.random.normal(ks[2], (E, H, D), jnp.float32) * s(D), 'w2': jax.random.normal(ks[3], (E, D, H), jnp.float32) * s(H), 'sfc1': jax.random.normal(ks[4], (S, D), jnp.float32) * s(D), 'sfc2': jax.random.normal(ks[5], (S, D), jnp.float32) * s(D), 'sfc3': jax.random.normal(ks[6], (D, S), jnp.float32) * s(S)}
    _L0_ffn_all = _L0_ffn_setup()
    _L0_ffn_in = {k: v for k, v in _L0_ffn_all.items() if k in ('gate_w', 'w1', 'w2', 'sfc1', 'sfc2', 'sfc3')}
    del _L0_ffn_all
    return {'x': x, 'ctx_1024': ctx_1024, 'itok_BxSx2_0_63': itok_BxSx2_0_63, 'L0_xattn_Wq': _L0_xattn_in['Wq'], 'L0_xattn_Wk': _L0_xattn_in['Wk'], 'L0_xattn_Wv': _L0_xattn_in['Wv'], 'L0_xattn_Wp': _L0_xattn_in['Wp'], 'L0_xattn_bp': _L0_xattn_in['bp'], 'L0_ffn_gate_w': _L0_ffn_in['gate_w'], 'L0_ffn_w1': _L0_ffn_in['w1'], 'L0_ffn_w2': _L0_ffn_in['w2'], 'L0_ffn_sfc1': _L0_ffn_in['sfc1'], 'L0_ffn_sfc2': _L0_ffn_in['sfc2'], 'L0_ffn_sfc3': _L0_ffn_in['sfc3']}

def reference(x, ctx_1024, itok_BxSx2_0_63, L0_xattn_Wq, L0_xattn_Wk, L0_xattn_Wv, L0_xattn_Wp, L0_xattn_bp, L0_ffn_gate_w, L0_ffn_w1, L0_ffn_w2, L0_ffn_sfc1, L0_ffn_sfc2, L0_ffn_sfc3):
    import jax
    import jax.numpy as jnp

    def _L0_xattn_ref(query, key, value, xpos, ypos, Wq, Wk, Wv, Wp, bp):
        import jax, jax.numpy as jnp
        import numpy as np
        DIM = 256
        NUM_HEADS = 16
        HEAD_DIM = DIM // NUM_HEADS
        SCALE = HEAD_DIM ** (-0.5)
        B, N, C = query.shape
        H, D = (NUM_HEADS, HEAD_DIM)
        q = (query @ Wq.T).reshape(B, N, H, D)
        k = (key @ Wk.T).reshape(B, N, H, D)
        v = (value @ Wv.T).reshape(B, N, H, D)
        attn = jnp.einsum('bnhd,bngd->bnhg', q, k) * SCALE
        attn = jax.nn.softmax(attn, axis=-1)
        x = jnp.einsum('bnhg,bngd->bnhd', attn, v)
        x = jnp.transpose(x, (0, 2, 1, 3)).reshape(B, N, C)
        return x @ Wp.T + bp

    def _L0_ffn_ref(x, gate_w, w1, w2, sfc1, sfc2, sfc3):
        import jax, jax.numpy as jnp
        import numpy as np
        TOP_K = 2
        B, L, D = x.shape
        E = gate_w.shape[0]
        shared = jnp.einsum('bls,ds->bld', jax.nn.silu(jnp.einsum('bld,sd->bls', x, sfc1)) * jnp.einsum('bld,sd->bls', x, sfc2), sfc3)
        logits = jnp.einsum('bld,ed->ble', x, gate_w)
        top_w, top_idx = jax.lax.top_k(logits, TOP_K)
        top_w = jax.nn.softmax(top_w, axis=-1)
        xf = x.reshape(-1, D)
        T = xf.shape[0]
        idx = top_idx.reshape(T, TOP_K)
        wk = top_w.reshape(T, TOP_K)
        dispatch = jnp.zeros((T, E), xf.dtype).at[jnp.arange(T)[:, None], idx].add(wk)
        h = jax.nn.silu(jnp.einsum('td,ehd->teh', xf, w1))
        moe = jnp.einsum('teh,te,edh->td', h, dispatch, w2)
        return moe.reshape(B, L, D) + shared
    x = x + _L0_xattn_ref(_layernorm(x, axis=-1), ctx_1024, ctx_1024, itok_BxSx2_0_63, itok_BxSx2_0_63, L0_xattn_Wq, L0_xattn_Wk, L0_xattn_Wv, L0_xattn_Wp, L0_xattn_bp)
    x = x + _L0_ffn_ref(_layernorm(x, axis=-1), L0_ffn_gate_w, L0_ffn_w1, L0_ffn_w2, L0_ffn_sfc1, L0_ffn_sfc2, L0_ffn_sfc3)
    return x

_drawn_inputs = setup_inputs


def setup_inputs(seed=0):
    import zlib

    import numpy as np

    out = dict(_drawn_inputs(seed))
    spreads = {}
    factors = {}
    for name, (base, spread) in spreads.items():
        noise = np.random.default_rng([zlib.crc32(name.encode()), seed]).standard_normal(out[name].shape)
        drawn = base * np.exp(spread * noise) if base else spread * noise
        out[name] = jnp.asarray(drawn.astype(out[name].dtype))
    for name, factor in factors.items():
        out[name] = (out[name] * factor).astype(out[name].dtype)
    return out
```

```python
import concourse.bass as bass
from concourse import mybir
from contextlib import ExitStack

B, N, C = 128, 128, 256
H, D = 16, 16
E, HID = 16, 128
SH = 512
P = 128
BPC = 4
TOK = BPC * N
CHUNKS = B // BPC
KT = C // P
GROUPS = TOK // 8
BANK = 512
SB_BLOCKS = SH // HID
STEPS = SB_BLOCKS + E
FIRST_HALF = STEPS // 2
SCALE = float(D) ** -0.5
EPS = 1e-5
Y_LAG = 2


def xattn_ffn_kernel(nc, x_in, x_res, ctx_t, wq, wkv, wp, bias, wgate, wsh, wsh_out, w1, w2,
                     ident_in, sel_in, mask_in, iota_in, out):
    f32, f32r, u32 = mybir.dt.float32, mybir.dt.float32r, mybir.dt.uint32
    ALU, ACT, AX = mybir.AluOpType, mybir.ActivationFunctionType, mybir.AxisListType

    ctx = ExitStack()
    with ctx:
        def sb(name, shape, dt=f32):
            return ctx.enter_context(nc.sbuf_tensor(name, shape, dt))

        def bank(name):
            return ctx.enter_context(nc.psum_tensor(name, [P, BANK], f32))

        def sem(name):
            return ctx.enter_context(nc.semaphore(name))

        q_dram = nc.dram_tensor("q_dram", [CHUNKS, P, BPC * C], f32).ap()
        kv_dram = nc.dram_tensor("kv_dram", [CHUNKS, P, BPC * 2 * C], f32).ap()

        wq_sb = sb("wq_sb", [P, KT, C])
        wkv_sb = sb("wkv_sb", [P, KT, 2 * C])
        wp_sb = sb("wp_sb", [P, KT, C])
        bias_sb = sb("bias_sb", [P, KT])
        wgate_sb = sb("wgate_sb", [P, KT, 32])
        wsh_sb = sb("wsh_sb", [P, KT, 2 * SH])
        wsh_out_sb = sb("wsh_out_sb", [P, SB_BLOCKS, C])
        w1_sb = sb("w1_sb", [P, KT, E * HID])
        w2_sb = sb("w2_sb", [P, E, C])
        ident = sb("ident", [P, P])
        sel = sb("sel", [P, E, P], f32r)
        quad_mask = sb("quad_mask", [P, BPC])
        iota = sb("iota", [P, E])

        x_sb = sb("x_sb", [P, BPC, C])
        xn_t = sb("xn_t", [P, KT, TOK])
        ctx_sb = sb("ctx_sb", [P, KT, TOK])
        q_sb = sb("q_sb", [P, BPC, C])
        xn = q_sb
        kv_sb = sb("kv_sb", [P, BPC, 2 * C])
        q_rows = sb("q_rows", [P, GROUPS, 32])
        k_diag = sb("k_diag", [P, GROUPS, 8, H])
        v_diag = sb("v_diag", [P, GROUPS, 8, D])
        prob = sb("prob", [P, 4, BANK])
        sel_f = prob[:, :, :].rearrange("p u (e f) -> p (u e) f", f=P)
        prob_t = sb("prob_t", [P, 4 * BANK])
        row_max = sb("row_max", [P, 4, 32])
        row_sum = sb("row_sum", [P, 4, 32])
        row_inv = sb("row_inv", [P, 4, 32])
        o_t = prob[:, :, :].rearrange("p u f -> p (u f)")
        res_t = sb("res_t", [P, 2, KT, TOK])
        xn2 = sb("xn2", [P, BPC, C])
        xn2_t = sb("xn2_t", [P, KT, TOK])
        turn_mark = sb("turn_mark", [P, 1])
        eps = sb("eps", [P, BPC])
        minus_half = sb("minus_half", [P, BPC])
        ln1_stats = sb("ln1_stats", [P, BPC, 6])
        ln1_mv = sb("ln1_mv", [P, BPC, 2])
        ln1_eps = sb("ln1_eps", [P, BPC])
        ln1_rstd = sb("ln1_rstd", [P, BPC])
        ln2_stats = sb("ln2_stats", [P, BPC, 6])
        ln2_mv = sb("ln2_mv", [P, BPC, 2])
        ln2_eps = sb("ln2_eps", [P, BPC])
        ln2_rstd = sb("ln2_rstd", [P, BPC])

        logits = sb("logits", [P, BPC, 32])
        top = sb("top", [P, BPC, 8])
        top_i = sb("top_i", [P, BPC, 8], u32)
        top_f = sb("top_f", [P, BPC, 8])
        gap = sb("gap", [P, BPC])
        gap_e = sb("gap_e", [P, BPC])
        gap_1 = sb("gap_1", [P, BPC])
        w_top = sb("w_top", [P, 2, BPC])
        hot = sb("hot", [P, 2, BPC, E])
        hot_w = sb("hot_w", [P, 2, BPC, E])
        gates = sb("gates", [P, BPC, E])
        gates_hi = sb("gates_hi", [P, BPC, E], f32r)
        gates_2 = sb("gates_2", [P, BPC, 32])
        gates_t = sb("gates_t", [P, P])
        gates_diag = sb("gates_diag", [P, BPC, P], f32r)

        th = sb("th", [P, 2, TOK])
        hid = sb("hid", [P, Y_LAG + 1, TOK])

        A = [bank(f"bank_a{i}") for i in range(3)]
        Z = [bank(f"bank_z{i}") for i in range(2)]
        U = bank("bank_u")
        Y = [bank(f"bank_y{i}") for i in range(KT)]

        names = """w_attn w_ffn const_in sel_ready zero_ready
            x_in_done ctx_done res_done q_stored kv_stored qk_read v_read out_stored
            ln1_step ln1_var ln1_eps ln1_pow xn_ready t1_full xn_t_ready kv_full kv_out q_full q_out
            s_full s_step s_shifted s_exp p_step p_ready o_full o_taken y_full h2_ready h2_full
            ln2_step ln2_var ln2_eps ln2_pow xn2_ready t2_full t2_out g_full g_out top_step gap_ready gap_exp gates_ready
            z_full z_tanh z_used u_full hid_ready hid_used acc_full out_ready""".split()
        S = {n: sem(n) for n in names}

        def at(per, c, k):
            return c * per + k

        def value(eng, v):
            return v if isinstance(v, int) else eng.snap(v)

        block = ctx.enter_context(nc.Block())

        @block.sync
        def _(sp):
            def chunk(c, first):
                if not first:
                    sp.wait_ge(S["kv_full"], at(4, c, 0))
                sp.dma_start(ctx_sb[:, :, :], ctx_t[c]).then_inc(S["ctx_done"], 16)
                if not first:
                    sp.wait_ge(S["xn_ready"], at(1, c, 0))
                sp.dma_start(x_sb[:, :, :], x_in[c]).then_inc(S["x_in_done"], 16)
                sp.wait_ge(S["kv_out"], at(4, c, 4))
                sp.dma_start(kv_dram[c], kv_sb[:, :, :]).then_inc(S["kv_stored"], 16)
                sp.wait_ge(S["q_out"], at(2, c, 2))
                sp.dma_start(q_dram[c], q_sb[:, :, :]).then_inc(S["q_stored"], 16)
                if first:
                    sp.wait_ge(S["zero_ready"], 5)
                else:
                    sp.wait_ge(S["s_full"], at(4, c, 0))
                sp.wait_ge(S["kv_stored"], at(16, c, 16))
                sp.wait_ge(S["q_stored"], at(16, c, 16))
                kv = kv_dram[c].rearrange("(t n) (i w f) -> t n i w f", t=8, i=BPC, w=2)
                q = q_dram[c].rearrange("(t n) (i f) -> t n i f", t=8, i=BPC)
                for pair in range(4):
                    for t2 in range(2):
                        src = t2 * 4 + pair
                        t = pair * 2 + t2
                        rows = slice(16 * t, 16 * t + 16)
                        sp.dma_start(k_diag[rows, :, t, :],
                                     kv[src, :, :, 0, :].rearrange("n i (d g) -> d (n i) g", d=D)).then_inc(S["qk_read"], 16)
                        sp.dma_start(q_rows[rows, :, 0:H],
                                     q[src].rearrange("n i (d h) -> d (n i) h", d=D)).then_inc(S["qk_read"], 16)
                if not first:
                    sp.wait_ge(S["o_full"], at(4, c, 0))
                kv_t2 = kv_dram[c].rearrange("(t m) (i w f) -> t m i w f", t=2, i=BPC, w=2)
                for i in range(BPC):
                    for t2 in range(2):
                        r = i * 2 + t2
                        sp.dma_start(v_diag[16 * r:16 * r + 16, :, r, :],
                                     kv_t2[t2, :, i, 1, :].rearrange("m (g d) -> g m d", g=H)).then_inc(S["v_read"], 16)

            chunk(0, True)
            with sp.Fori(1, CHUNKS) as c:
                chunk(c, False)

        @block.gpsimd
        def _(pool):
            nc.gpsimd.memset(eps[:, :], EPS).then_inc(S["zero_ready"], 1)
            nc.gpsimd.memset(minus_half[:, :], -0.5).then_inc(S["zero_ready"], 1)
            nc.gpsimd.memset(q_rows[:, :, :], 0.0).then_inc(S["zero_ready"], 1)
            nc.gpsimd.memset(v_diag[:, :, :, :], 0.0).then_inc(S["zero_ready"], 1)

            def ln1_power(c):
                pool.wait_ge(S["ln1_var"], at(1, c, 1))
                nc.gpsimd.tensor_tensor(ln1_eps[:, :], ln1_mv[:, :, 1], eps[:, :], ALU.add).then_inc(S["ln1_eps"], 1)
                pool.wait_ge(S["ln1_eps"], at(1, c, 1))
                nc.gpsimd.tensor_tensor(ln1_rstd[:, :], ln1_eps[:, :], minus_half[:, :], ALU.pow).then_inc(S["ln1_pow"], 1)

            def load_residual(c, par):
                pool.dma_start(res_t[:, par, :, :], x_res[c]).then_inc(S["res_done"], 16)

            def ln2_power(c):
                pool.wait_ge(S["ln2_var"], at(1, c, 1))
                nc.gpsimd.tensor_tensor(ln2_eps[:, :], ln2_mv[:, :, 1], eps[:, :], ALU.add).then_inc(S["ln2_eps"], 1)
                pool.wait_ge(S["ln2_eps"], at(1, c, 1))
                nc.gpsimd.tensor_tensor(ln2_rstd[:, :], ln2_eps[:, :], minus_half[:, :], ALU.pow).then_inc(S["ln2_pow"], 1)

            def store(c, par):
                pool.wait_ge(S["out_ready"], at(2, c, 2))
                pool.dma_start(out[c], res_t[:, par, :, :]).then_inc(S["out_stored"], 16)

            load_residual(0, 0)
            pool.wait_ge(S["zero_ready"], 5)
            ln1_power(0)
            ln1_power(1)
            ln2_power(0)
            ln1_power(2)
            pool.wait_ge(S["res_done"], 16)
            load_residual(1, 1)

            def body(c, par, ahead, load):
                ln2_power(c)
                store(c - 1, 1 - par)
                if ahead:
                    ln1_power(c + 2)
                if load:
                    pool.wait_ge(S["out_stored"], at(16, c, 0))
                    load_residual(c + 1, 1 - par)

            body(1, 1, True, True)
            with pool.Fori(2, CHUNKS - 2, 2) as c:
                body(c, 0, True, True)
                body(c + 1, 1, True, True)
            body(CHUNKS - 2, 0, False, True)
            body(CHUNKS - 1, 1, False, False)
            store(CHUNKS - 1, 1)
            pool.wait_ge(S["out_stored"], 16 * CHUNKS)

        @block.scalar
        def _(act):
            for dst, src in ((wkv_sb, wkv), (wq_sb, wq), (wp_sb, wp), (bias_sb, bias)):
                act.dma_start(dst[:], src).then_inc(S["w_attn"], 16)
            for dst, src in ((ident, ident_in), (quad_mask, mask_in), (iota, iota_in), (sel_f, sel_in)):
                act.dma_start(dst if dst is sel_f else dst[:], src).then_inc(S["const_in"], 16)
            for dst, src in ((wgate_sb, wgate), (wsh_sb, wsh), (wsh_out_sb, wsh_out), (w1_sb, w1), (w2_sb, w2)):
                act.dma_start(dst[:], src).then_inc(S["w_ffn"], 16)

            def exps(c):
                for u in range(4):
                    act.wait_ge(S["s_shifted"], at(4, c, u + 1))
                    nc.scalar.activation(prob[:, u, :], prob[:, u, :], ACT.Exp).then_inc(S["s_exp"], 1)

            def project_out(c, first):
                for k in range(KT):
                    act.wait_ge(S["t1_full"], at(KT, c, k + 1))
                    nc.scalar.activation(xn_t[:, k, :], A[1 + k][:, :], ACT.Copy).then_inc(S["xn_t_ready"], 1)
                if not first:
                    act.wait_ge(S["kv_stored"], at(16, c, 0))
                    act.wait_ge(S["q_stored"], at(16, c, 0))
                for i in range(BPC):
                    act.wait_ge(S["kv_full"], at(4, c, i + 1))
                    nc.scalar.activation(kv_sb[:, i, :], A[i % 3][:, :], ACT.Copy).then_inc(S["kv_out"], 1)
                for i in range(2):
                    act.wait_ge(S["q_full"], at(2, c, i + 1))
                    nc.scalar.activation(q_sb[:, 2 * i:2 * i + 2, :].rearrange("p i f -> p (i f)"), A[1 + i][:, :],
                                         ACT.Copy, scale=SCALE).then_inc(S["q_out"], 1)

            def tanhs(c, steps, first=False):
                for s in steps:
                    act.wait_ge(S["z_full"], at(STEPS, c, s + 1))
                    if s >= 2:
                        act.wait_ge(S["hid_ready"], at(STEPS, c, s - 1))
                    elif not first:
                        act.wait_ge(S["hid_ready"], at(STEPS, c, 0))
                    nc.scalar.activation(th[:, s % 2, :], Z[s % 2][:, :], ACT.Tanh, scale=0.5).then_inc(S["z_tanh"], 1)

            def transposes_out(c):
                for k in range(KT):
                    act.wait_ge(S["t2_full"], at(KT, c, k + 1))
                    nc.scalar.activation(xn2_t[:, k, :], A[(2, 0)[k]][:, :], ACT.Copy).then_inc(S["t2_out"], 1)

            def gap_exps(c):
                act.wait_ge(S["gap_ready"], at(1, c, 1))
                nc.scalar.activation(gap_e[:, :], gap[:, :], ACT.Exp).then_inc(S["gap_exp"], 1)

            project_out(0, True)
            exps(0)
            project_out(1, False)
            transposes_out(0)
            gap_exps(0)
            def body(c, first):
                exps(c)
                project_out(c + 1, False)
                tanhs(c - 1, range(STEPS), first)
                transposes_out(c)
                gap_exps(c)

            body(1, True)
            with act.Fori(2, CHUNKS - 1) as c:
                body(c, False)
            exps(CHUNKS - 1)
            tanhs(CHUNKS - 2, range(STEPS))
            transposes_out(CHUNKS - 1)
            gap_exps(CHUNKS - 1)
            tanhs(CHUNKS - 1, range(STEPS))

        @block.vector
        def _(dve):
            nc.vector.memset(k_diag[:, :, :, :], 0.0).then_inc(S["zero_ready"], 1)
            dve.wait_ge(S["const_in"], 16 * 4)
            nc.vector.tensor_copy(sel[:, :, :], sel_f).then_inc(S["sel_ready"], 1)

            LN_STEPS, TOP_STEPS, S_STEPS, P_STEPS = 2, 8, 4, 9

            def ln1(c, first):
                dve.wait_ge(S["x_in_done"], at(16, c, 16))
                if not first:
                    dve.wait_ge(S["q_stored"], at(16, c, 0))
                for i in range(BPC):
                    st = nc.vector.bn_stats(ln1_stats[:, i, :], x_sb[:, i, :])
                st.then_inc(S["ln1_step"], 1)
                dve.wait_ge(S["ln1_step"], at(1, c, 1))
                nc.vector.memset(turn_mark[:, :], 0.0)
                for i in range(BPC):
                    st = nc.vector.bn_aggr(ln1_mv[:, i, :], ln1_stats[:, i, :])
                st.then_inc(S["ln1_var"], 1)
                dve.wait_ge(S["ln1_pow"], at(1, c, 1))
                for i in range(BPC):
                    st = nc.vector.tensor_scalar(xn[:, i, :], x_sb[:, i, :], ln1_mv[:, i, 0:1], ln1_rstd[:, i:i + 1],
                                                 ALU.subtract, ALU.mult)
                st.then_inc(S["xn_ready"], 1)

            def softmax(c, first):
                def shift(u):
                    dve.wait_ge(S["s_step"], at(4, c, u + 1))
                    sc = A[u % 3][:, :].rearrange("p (t g) -> p t g", g=H)
                    nc.vector.tensor_tensor(prob[:, u, :].rearrange("p (t g) -> p t g", g=H), sc,
                                            row_max[:, u, :].unsqueeze(2).to_broadcast([P, 32, H]),
                                            ALU.subtract).then_inc(S["s_shifted"], 1)

                for u in range(4):
                    if u == 3:
                        shift(1)
                        shift(2)
                    dve.wait_ge(S["s_full"], at(4, c, u + 1))
                    nc.vector.tensor_reduce(row_max[:, u, :], A[u % 3][:, :].rearrange("p (t g) -> p t g", g=H),
                                            AX.X, ALU.max).then_inc(S["s_step"], 1)
                    if u == 1:
                        shift(0)
                shift(3)
                for u in range(4):
                    dve.wait_ge(S["s_exp"], at(4, c, u + 1))
                    nc.vector.tensor_reduce(row_sum[:, u, :], prob[:, u, :].rearrange("p (t g) -> p t g", g=H),
                                            AX.X, ALU.add).then_inc(S["p_step"], 1)
                dve.wait_ge(S["p_step"], at(P_STEPS, c, 4))
                nc.vector.reciprocal(row_inv[:, :, :], row_sum[:, :, :]).then_inc(S["p_step"], 1)
                dve.wait_ge(S["p_step"], at(P_STEPS, c, 5))
                for u in range(4):
                    pr = prob[:, u, :].rearrange("p (t g) -> p t g", g=H)
                    nc.vector.tensor_tensor(pr, pr, row_inv[:, u, :].unsqueeze(2).to_broadcast([P, 32, H]),
                                            ALU.mult).then_inc(S["p_step"], 1)
                for u in range(4):
                    dve.wait_ge(S["p_step"], at(P_STEPS, c, 6 + u))
                    nc.vector.transpose(prob_t[:, u * BANK:(u + 1) * BANK], prob[:, u, :]).then_inc(S["p_ready"], 1)

            def ffn_act(c, steps, last):
                def first_part(s):
                    dve.wait_ge(S["z_tanh"], at(STEPS, c, s + 1))
                    nc.vector.scalar_tensor_tensor(out=th[:, s % 2, :], in0=th[:, s % 2, :], scalar=1.0,
                                                   in1=Z[s % 2][:, :], op0=ALU.add, op1=ALU.mult).then_inc(S["z_used"], 1)

                def second_part(s):
                    dve.wait_ge(S["z_used"], at(STEPS, c, s + 1))
                    dve.wait_ge(S["u_full"], at(STEPS, c, s + 1))
                    if s > Y_LAG:
                        dve.wait_ge(S["hid_used"], at(STEPS, c, s - Y_LAG))
                    nc.vector.scalar_tensor_tensor(out=hid[:, s % (Y_LAG + 1), :], in0=th[:, s % 2, :], scalar=0.5,
                                                   in1=U[:, :], op0=ALU.mult, op1=ALU.mult).then_inc(S["hid_ready"], 1)

                for s in steps:
                    first_part(s)
                    if s > 0:
                        second_part(s - 1)
                if last:
                    second_part(STEPS - 1)

            def attention_out(c):
                for u in range(4):
                    dve.wait_ge(S["o_full"], at(4, c, u + 1))
                    nc.vector.transpose(o_t[:, u * BANK:(u + 1) * BANK], A[u % 3][:, :]).then_inc(S["o_taken"], 1)

            def residual(c, par):
                dve.wait_ge(S["res_done"], at(16, c, 16))
                for k in range(KT):
                    dve.wait_ge(S["y_full"], at(KT, c, k + 1))
                    nc.vector.scalar_tensor_tensor(out=res_t[:, par, k, :], in0=A[1 + k][:, :], scalar=bias_sb[:, k:k + 1],
                                                   in1=res_t[:, par, k, :], op0=ALU.add, op1=ALU.add).then_inc(S["h2_ready"], 1)

            def ln2_moments(c):
                for i in range(BPC):
                    if i % 2 == 0:
                        dve.wait_ge(S["h2_full"], at(2, c, i // 2 + 1))
                    st = nc.vector.bn_stats(ln2_stats[:, i, :], A[i // 2][:, i % 2 * C:(i % 2 + 1) * C])
                st.then_inc(S["ln2_step"], 1)
                dve.wait_ge(S["ln2_step"], at(1, c, 1))
                nc.vector.memset(turn_mark[:, :], 0.0)
                for i in range(BPC):
                    st = nc.vector.bn_aggr(ln2_mv[:, i, :], ln2_stats[:, i, :])
                st.then_inc(S["ln2_var"], 1)

            def ln2(c):
                dve.wait_ge(S["ln2_pow"], at(1, c, 1))
                for i in range(BPC):
                    st = nc.vector.tensor_scalar(xn2[:, i, :], A[i // 2][:, i % 2 * C:(i % 2 + 1) * C],
                                                 ln2_mv[:, i, 0:1], ln2_rstd[:, i:i + 1], ALU.subtract, ALU.mult)
                st.then_inc(S["xn2_ready"], 1)

            def final_sum(c, par):
                dve.wait_ge(S["acc_full"], at(1, c, 1))
                for k in range(KT):
                    nc.vector.tensor_tensor(res_t[:, par, k, :], Y[k][:, :], res_t[:, par, k, :], ALU.add).then_inc(S["out_ready"], 1)

            def route(c):
                dve.wait_ge(S["g_full"], at(1, c, 1))
                nc.vector.transpose(logits[:, :, :].rearrange("p b e -> p (b e)"), A[1][:, 0:P]).then_inc(S["g_out"], 1)
                turned = value(dve, at(1, c, 1))
                dve.wait_ge(S["const_in"], 16 * 4)
                dve.wait_ge(S["g_out"], turned)
                for b in range(BPC):
                    st = nc.vector.max(top[:, b, :], logits[:, b, 0:E])
                st.then_inc(S["top_step"], 1)
                dve.wait_ge(S["top_step"], at(TOP_STEPS, c, 1))
                nc.vector.tensor_tensor(gap[:, :], top[:, :, 1], top[:, :, 0], ALU.subtract).then_inc(S["gap_ready"], 1)
                for b in range(BPC):
                    st = nc.vector.max_index(top_i[:, b, :], top[:, b, :], logits[:, b, 0:E])
                st.then_inc(S["top_step"], 1)
                dve.wait_ge(S["top_step"], at(TOP_STEPS, c, 2))
                nc.vector.tensor_copy(top_f[:, :, :], top_i[:, :, :]).then_inc(S["top_step"], 1)
                dve.wait_ge(S["gap_exp"], at(1, c, 1))
                nc.vector.tensor_scalar(gap_1[:, :], gap_e[:, :], 1.0, None, ALU.add).then_inc(S["top_step"], 1)
                dve.wait_ge(S["top_step"], at(TOP_STEPS, c, 4))
                for j in range(2):
                    st = nc.vector.tensor_tensor(hot[:, j], iota[:, :].unsqueeze(1).to_broadcast([P, BPC, E]),
                                                 top_f[:, :, j].unsqueeze(2).to_broadcast([P, BPC, E]), ALU.is_equal)
                nc.vector.reciprocal(w_top[:, 0, :], gap_1[:, :]).then_inc(S["top_step"], 1)
                dve.wait_ge(S["top_step"], at(TOP_STEPS, c, 5))
                nc.vector.tensor_tensor(w_top[:, 1, :], gap_e[:, :], w_top[:, 0, :], ALU.mult).then_inc(S["top_step"], 1)
                dve.wait_ge(S["top_step"], at(TOP_STEPS, c, 6))
                for j in range(2):
                    st = nc.vector.tensor_tensor(hot_w[:, j], hot[:, j],
                                                 w_top[:, j, :].unsqueeze(2).to_broadcast([P, BPC, E]), ALU.mult)
                st.then_inc(S["top_step"], 1)
                dve.wait_ge(S["top_step"], at(TOP_STEPS, c, 7))
                nc.vector.tensor_tensor(gates[:, :, :], hot_w[:, 0], hot_w[:, 1], ALU.add).then_inc(S["top_step"], 1)

            def spread_gates(c, first):
                G = 4
                dve.wait_ge(S["top_step"], at(TOP_STEPS, c, 8))
                nc.vector.tensor_copy(gates_hi[:, :, :], gates[:, :, :]).then_inc(S["gates_ready"], 1)
                dve.wait_ge(S["gates_ready"], at(G, c, 1))
                nc.vector.tensor_copy(gates_2[:, :, 0:E], gates_hi[:, :, :].bitcast(f32))
                nc.vector.tensor_tensor(gates_2[:, :, E:2 * E], gates[:, :, :], gates_hi[:, :, :].bitcast(f32),
                                        ALU.subtract).then_inc(S["gates_ready"], 1)
                dve.wait_ge(S["gates_ready"], at(G, c, 2))
                nc.vector.transpose(gates_t[:, :], gates_2[:, :, :].rearrange("p b e -> p (b e)")).then_inc(S["gates_ready"], 1)
                dve.wait_ge(S["gates_ready"], at(G, c, 3))
                nc.vector.tensor_tensor(gates_diag[:, :, :], gates_t[:, :].unsqueeze(1).to_broadcast([P, BPC, P]),
                                        quad_mask[:, :].unsqueeze(2).to_broadcast([P, BPC, P]), ALU.mult).then_inc(S["gates_ready"], 1)

            ln1(0, True)
            ln1(1, False)
            softmax(0, True)
            attention_out(0)
            residual(0, 0)
            ln2_moments(0)
            ln2(0)
            route(0)
            spread_gates(0, True)
            ln1(2, False)

            def body(c, par, ahead):
                softmax(c, False)
                ffn_act(c - 1, range(FIRST_HALF), False)
                attention_out(c)
                residual(c, par)
                ffn_act(c - 1, range(FIRST_HALF, FIRST_HALF + 2), False)
                ln2_moments(c)
                ffn_act(c - 1, range(FIRST_HALF + 2, STEPS - 2), False)
                ln2(c)
                ffn_act(c - 1, range(STEPS - 2, STEPS), True)
                final_sum(c - 1, 1 - par)
                route(c)
                spread_gates(c, False)
                if ahead:
                    ln1(c + 2, False)

            body(1, 1, True)
            with dve.Fori(2, CHUNKS - 2, 2) as c:
                body(c, 0, True)
                body(c + 1, 1, True)
            body(CHUNKS - 2, 0, False)
            body(CHUNKS - 1, 1, False)
            ffn_act(CHUNKS - 1, range(STEPS), True)
            final_sum(CHUNKS - 1, 1)

        @block.tensor
        def _(pe):
            mm = nc.tensor.matmul

            def scores(c, first):
                pe.wait_ge(S["qk_read"], at(256, c, 256))
                if not first:
                    pe.wait_ge(S["t2_out"], at(KT, c, 0))
                    pe.wait_ge(S["g_out"], at(1, c, 0))
                for u in range(4):
                    if u == 3:
                        pe.wait_ge(S["s_shifted"], at(4, c, 1))
                    for n in range(4):
                        for a in range(4):
                            m = (u * 4 + n) * 4 + a
                            last = mm(A[u % 3][32 * a:32 * a + 32, n * P:(n + 1) * P], q_rows[:, m, :],
                                      k_diag[:, m, :, :].rearrange("p t g -> p (t g)"), start=True, stop=True)
                    last.then_inc(S["s_full"], 1)

            def project(c, first):
                pe.wait_ge(S["xn_ready"], at(1, c, 1))
                for k in range(KT):
                    if not first:
                        pe.wait_ge(S["s_shifted"], at(4, c - 1, 2 + k))
                    for i in range(BPC):
                        last = nc.tensor.transpose(A[1 + k][:, i * P:(i + 1) * P], xn[:, i, k * P:(k + 1) * P], ident[:, :])
                    last.then_inc(S["t1_full"], 1)
                pe.wait_ge(S["ctx_done"], at(16, c, 16))
                for i in range(BPC):
                    if i == 0 and not first:
                        pe.wait_ge(S["s_shifted"], at(4, c - 1, 4))
                    if i in (1, 2):
                        pe.wait_ge(S["xn_t_ready"], at(KT, c, i))
                    if i == 3:
                        pe.wait_ge(S["kv_out"], at(4, c, 1))
                    for k in range(KT):
                        last = mm(A[i % 3][:, :], ctx_sb[:, k, i * P:(i + 1) * P], wkv_sb[:, k, :],
                                  start=k == 0, stop=k == KT - 1)
                    last.then_inc(S["kv_full"], 1)
                for i in range(2):
                    pe.wait_ge(S["kv_out"], at(4, c, 2 + i))
                    for j in range(2):
                        t = 2 * i + j
                        for k in range(KT):
                            last = mm(A[1 + i][:, j * C:(j + 1) * C], xn_t[:, k, t * P:(t + 1) * P], wq_sb[:, k, :],
                                      start=k == 0, stop=k == KT - 1)
                    last.then_inc(S["q_full"], 1)

            def attend(c, behind):
                pe.wait_ge(S["v_read"], at(128, c, 128))
                for u in range(4):
                    pe.wait_ge(S["p_ready"], at(4, c, u + 1))
                    if u == 3:
                        pe.wait_ge(S["o_taken"], at(4, c, 1))
                    elif behind:
                        pe.wait_ge(S["kv_out" if u == 0 else "q_out"], at(4, c + 1, 4) if u == 0 else at(2, c + 1, u))
                    for n in range(4):
                        for pair in range(4):
                            g = (u * 4 + n) * 4 + pair
                            last = mm(A[u % 3][32 * pair:32 * pair + 32, n * P:(n + 1) * P],
                                      prob_t[:, 32 * g:32 * g + 32],
                                      v_diag[:, pair * 16 + u * 4 + n, :, :].rearrange("p t d -> p (t d)"), start=True, stop=True)
                    last.then_inc(S["o_full"], 1)
                pe.wait_ge(S["o_taken"], at(4, c, 4))
                cols = o_t.rearrange("p (j n i h) -> p j i n h", j=2, n=8, i=BPC)
                for k in range(KT):
                    for j in range(2):
                        last = mm(A[1 + k][:, :], wp_sb[:, j, k * P:(k + 1) * P], cols[:, j, :, :, 0:H], start=j == 0, stop=j == 1)
                    last.then_inc(S["y_full"], 1)

            def back(c, par):
                pe.wait_ge(S["h2_ready"], at(KT, c, KT))
                for i in range(BPC):
                    for k in range(KT):
                        last = nc.tensor.transpose(A[i // 2][:, i % 2 * C + k * P:i % 2 * C + (k + 1) * P],
                                                   res_t[:, par, k, i * P:(i + 1) * P], ident[:, :])
                    if i % 2:
                        last.then_inc(S["h2_full"], 1)

            def turn(c):
                pe.wait_ge(S["xn2_ready"], at(1, c, 1))
                for k in range(KT):
                    for i in range(BPC):
                        last = nc.tensor.transpose(A[(2, 0)[k]][:, i * P:(i + 1) * P], xn2[:, i, k * P:(k + 1) * P], ident[:, :])
                    last.then_inc(S["t2_full"], 1)
                pe.wait_ge(S["t2_out"], at(KT, c, KT))
                for i in range(BPC):
                    for k in range(KT):
                        last = mm(A[1][32 * i:32 * i + 32, 0:P], wgate_sb[:, k, :], xn2_t[:, k, i * P:(i + 1) * P],
                                  start=k == 0, stop=k == KT - 1)
                last.then_inc(S["g_full"], 1)

            def down(c, s):
                pe.wait_ge(S["hid_ready"], at(STEPS, c, s + 1))
                w = wsh_out_sb[:, s, :] if s < SB_BLOCKS else w2_sb[:, s - SB_BLOCKS, :]
                for k in range(KT):
                    last = mm(Y[k][:, :], w[:, k * P:(k + 1) * P], hid[:, s % (Y_LAG + 1), :],
                              start=s == 0, stop=s == STEPS - 1)
                last.then_inc(S["hid_used"], 1)
                if s == STEPS - 1:
                    pe.wait_ge(S["hid_used"], at(STEPS, c, STEPS))
                    pe.sem_inc(S["acc_full"], 1)

            def ffn(c, steps, first, last_half):
                if 0 in steps:
                    pe.wait_ge(S["gates_ready"], at(4, c, 4))
                    if not first:
                        pe.wait_ge(S["out_ready"], at(2, c, 0))
                for s in steps:
                    if s >= 2:
                        pe.wait_ge(S["z_used"], at(STEPS, c, s - 1))
                    for k in range(KT):
                        w = wsh_sb[:, k, s * HID:(s + 1) * HID] if s < SB_BLOCKS else \
                            w1_sb[:, k, (s - SB_BLOCKS) * HID:(s - SB_BLOCKS + 1) * HID]
                        last = mm(Z[s % 2][:, :], w, xn2_t[:, k, :], start=k == 0, stop=k == KT - 1)
                    last.then_inc(S["z_full"], 1)
                    if s >= Y_LAG:
                        down(c, s - Y_LAG)
                    if s >= 1:
                        pe.wait_ge(S["hid_ready"], at(STEPS, c, s))
                    if s < SB_BLOCKS:
                        for k in range(KT):
                            last = mm(U[:, :], wsh_sb[:, k, SH + s * HID:SH + (s + 1) * HID], xn2_t[:, k, :],
                                      start=k == 0, stop=k == KT - 1)
                    else:
                        last = mm(U[:, :], sel[:, s - SB_BLOCKS, :], gates_diag[:, :, :].rearrange("p b t -> p (b t)"),
                                  start=True, stop=True)
                    last.then_inc(S["u_full"], 1)
                if last_half:
                    for s in range(STEPS - Y_LAG, STEPS):
                        down(c, s)

            pe.wait_ge(S["w_attn"], 16 * 4)
            pe.wait_ge(S["const_in"], 16 * 4)
            project(0, True)
            scores(0, True)
            project(1, False)
            attend(0, True)
            pe.wait_ge(S["w_ffn"], 16 * 5)
            pe.wait_ge(S["sel_ready"], 1)
            back(0, 0)
            turn(0)

            def body(c, par, f_first, ahead):
                scores(c, False)
                if ahead:
                    project(c + 1, False)
                ffn(c - 1, range(FIRST_HALF), f_first, False)
                attend(c, ahead)
                ffn(c - 1, range(FIRST_HALF, FIRST_HALF + 2), f_first, False)
                back(c, par)
                ffn(c - 1, range(FIRST_HALF + 2, STEPS), f_first, True)
                turn(c)

            body(1, 1, True, True)
            with pe.Fori(2, CHUNKS - 2, 2) as c:
                body(c, 0, False, True)
                body(c + 1, 1, False, True)
            body(CHUNKS - 2, 0, False, True)
            body(CHUNKS - 1, 1, False, False)
            ffn(CHUNKS - 1, range(STEPS), False, True)


def kernel(**inputs):
    import numpy as np
    import concourse.bacc as bacc
    from concourse import mybir as mb
    from concourse.bass_utils import run_bass_kernel_spmd

    a = {k: np.asarray(v) for k, v in inputs.items()}
    x, c_in = a["x"], a["ctx_1024"]
    x7 = x.reshape(CHUNKS, BPC, 8, 2, 4, 2, C)
    c7 = c_in.reshape(CHUNKS, BPC, 8, 2, 4, 2, KT, P)
    heads = lambda w: w.T.reshape(C, H, D)
    by_k = lambda w: w.reshape(KT, P, -1).transpose(1, 0, 2)
    wq = heads(a["L0_xattn_Wq"]).transpose(0, 2, 1).reshape(C, C)
    wk = heads(a["L0_xattn_Wk"]).transpose(0, 2, 1).reshape(C, C)
    wv = a["L0_xattn_Wv"].T
    gate = np.zeros((C, 32), np.float32)
    gate[:, :E] = a["L0_ffn_gate_w"].T
    sel = np.zeros((P, E, P), np.float32)
    mask = np.zeros((P, BPC), np.float32)
    for p in range(P):
        sel[p, p % E, :] = 1.0
        mask[p, p // 32] = 1.0
    arrays = {
        "x_in": x7.transpose(0, 5, 4, 3, 2, 1, 6).reshape(CHUNKS, P, BPC, C),
        "x_res": x.reshape(CHUNKS, BPC, H, 8, KT, P).transpose(0, 5, 4, 1, 3, 2).reshape(CHUNKS, P, KT, TOK),
        "ctx_t": c7.transpose(0, 7, 6, 1, 5, 4, 3, 2).reshape(CHUNKS, P, KT, TOK),
        "wq": by_k(wq),
        "wkv": by_k(np.concatenate([wk, wv], axis=1)),
        "wp": by_k(a["L0_xattn_Wp"].T),
        "bias": a["L0_xattn_bp"].reshape(KT, P).T,
        "wgate": by_k(gate),
        "wsh": by_k(np.concatenate([a["L0_ffn_sfc1"].T, a["L0_ffn_sfc2"].T], axis=1)),
        "wsh_out": a["L0_ffn_sfc3"].T.reshape(SB_BLOCKS, P, C).transpose(1, 0, 2),
        "w1": by_k(a["L0_ffn_w1"].reshape(E * HID, C).T),
        "w2": a["L0_ffn_w2"].transpose(2, 0, 1),
        "ident": np.eye(P, dtype=np.float32),
        "sel": sel,
        "mask": mask,
        "iota": np.broadcast_to(np.arange(E, dtype=np.float32), (P, E)),
    }
    nc = bacc.Bacc("TRN2", target_bir_lowering=False, num_devices=1)
    given, args = {}, []
    for name, v in arrays.items():
        given[f"in_{name}"] = np.ascontiguousarray(v)
        args.append(nc.dram_tensor(f"in_{name}", v.shape, mb.dt.float32, kind="ExternalInput").ap())
    args.append(nc.dram_tensor("out_0", (CHUNKS, P, KT, TOK), mb.dt.float32, kind="ExternalOutput").ap())
    xattn_ffn_kernel(nc, *args)
    r = run_bass_kernel_spmd(nc, [given], core_ids=[0])
    got = np.asarray(r.results[0]["out_0"]).reshape(CHUNKS, P, KT, BPC, 8, H)
    return np.ascontiguousarray(got.transpose(0, 3, 5, 4, 2, 1)).reshape(B, N, C)
```

```python
import concourse.bass as bass
from concourse import mybir
from contextlib import ExitStack

B, N, C = 128, 128, 256
H, D = 16, 16
E, HID = 16, 128
TOP = 2
SH = 512
P = 128
BPC = 4
TOK = BPC * N
CHUNKS = B // BPC
TOKENS = B * N
KT = C // P
GROUPS = TOK // 8
BANK = 512
SB = SH // HID
SLOTS = TOP * BPC
TILES = TOP * TOKENS // P + E - 1
QUADS = -(-TILES // 4)
QUADS += -QUADS % 4
TILE_COLS = -(-QUADS * 4 // P)
CAP = TOKENS
NO_TILE = E * CAP // P
SCALE = float(D) ** -0.5
EPS = 1e-5


def xattn_ffn_kernel(nc, x_in, x_res, ctx_t, wq, wkv, wp, bias, wgate, wsh, wsh_out, w1, w2,
                     ident_in, before_in, iota_in, row_id_in, tile_id_in, out):
    f32, bf16, i32, u32 = mybir.dt.float32, mybir.dt.bfloat16, mybir.dt.int32, mybir.dt.uint32
    ALU, ACT, AX = mybir.AluOpType, mybir.ActivationFunctionType, mybir.AxisListType

    ctx = ExitStack()
    with ctx:
        def sb(name, shape, dt=f32):
            return ctx.enter_context(nc.sbuf_tensor(name, shape, dt))

        def bank(name):
            return ctx.enter_context(nc.psum_tensor(name, [P, BANK], f32))

        def sem(name):
            return ctx.enter_context(nc.semaphore(name))

        q_dram = nc.dram_tensor("q_dram", [CHUNKS, P, BPC * C], f32).ap()
        kv_dram = nc.dram_tensor("kv_dram", [CHUNKS, P, BPC * 2 * C], f32).ap()
        normed = nc.dram_tensor("normed", [TOKENS, C], f32).ap()
        base = nc.dram_tensor("base", [CHUNKS, P, BPC * C], f32).ap()
        table = nc.dram_tensor("table", [(NO_TILE + 1) * P, 1], u32).ap()
        expert_out = nc.dram_tensor("expert_out", [QUADS * 4 * P, C], f32).ap()

        wq_sb = sb("wq_sb", [P, KT, C])
        wkv_sb = sb("wkv_sb", [P, KT, 2 * C])
        wp_sb = sb("wp_sb", [P, KT, C])
        bias_sb = sb("bias_sb", [P, KT])
        wgate_sb = sb("wgate_sb", [P, KT, 32])
        wsh_sb = sb("wsh_sb", [P, KT, 2 * SH])
        wsh_out_sb = sb("wsh_out_sb", [P, SB, C])
        w1_sb = sb("w1_sb", [P, KT, E * HID])
        w2_sb = sb("w2_sb", [P, E * C])
        ident = sb("ident", [P, P])
        before = sb("before", [P, P], bf16)
        ones = sb("ones", [P, P], bf16)
        iota = sb("iota", [P, E])
        row_id = sb("row_id", [P, BPC])
        tile_id = sb("tile_id", [P, TILE_COLS])
        eps = sb("eps", [P, BPC])
        minus_half = sb("minus_half", [P, BPC])
        turn_mark = sb("turn_mark", [P, 1])
        pool_mark = sb("pool_mark", [P, 8])

        x_sb = sb("x_sb", [P, BPC, C])
        xn_t = sb("xn_t", [P, KT, TOK])
        ctx_sb = sb("ctx_sb", [P, KT, TOK])
        q_sb = sb("q_sb", [P, BPC, C])
        xn = q_sb
        kv_sb = sb("kv_sb", [P, BPC, 2 * C])
        q_rows = sb("q_rows", [P, GROUPS, 32])
        k_diag = sb("k_diag", [P, GROUPS, 8, H])
        v_diag = sb("v_diag", [P, GROUPS, 8, D])
        prob = sb("prob", [P, 4, BANK])
        o_t = prob[:, :, :].rearrange("p u f -> p (u f)")
        prob_t = sb("prob_t", [P, 4 * BANK])
        before_f = prob_t[:, 0:P]
        row_max = sb("row_max", [P, 4, 32])
        row_sum = sb("row_sum", [P, 4, 32])
        row_inv = sb("row_inv", [P, 4, 32])
        res_t = sb("res_t", [P, KT, TOK])
        h2 = sb("h2", [P, 2, BPC, C])
        xn2 = sb("xn2", [P, BPC, C])
        xn2_t = sb("xn2_t", [P, KT, TOK])
        ln1_stats = sb("ln1_stats", [P, BPC, 6])
        ln1_mv = sb("ln1_mv", [P, BPC, 2])
        ln1_eps = sb("ln1_eps", [P, BPC])
        ln1_rstd = sb("ln1_rstd", [P, BPC])
        ln2_stats = sb("ln2_stats", [P, BPC, 6])
        ln2_mv = sb("ln2_mv", [P, BPC, 2])
        ln2_eps = sb("ln2_eps", [P, BPC])
        ln2_rstd = sb("ln2_rstd", [P, BPC])
        th = sb("th", [P, 2, TOK])
        hid = sb("hid", [P, SB, TOK])

        logits = sb("logits", [P, BPC, 32])
        top = sb("top", [P, BPC, 8])
        top_i = sb("top_i", [P, BPC, 8], u32)
        top_f = sb("top_f", [P, TOP, BPC])
        hot = sb("hot", [P, TOP, BPC, E], bf16)
        hot_new = sb("hot_new", [P, E])
        hot_sum = sb("hot_sum", [P, E], bf16)
        hot_pos = sb("hot_pos", [P, SLOTS, E])
        slot_f = sb("slot_f", [P, SLOTS])
        slot_i = sb("slot_i", [P, 2, SLOTS], u32)
        row_i = sb("row_i", [P, 2, BPC], u32)
        gap = sb("gap", [P, BPC])
        gap_e = sb("gap_e", [P, BPC])
        gap_1 = sb("gap_1", [P, BPC])
        half_inv = sb("half_inv", [P, BPC])
        expert_rec = sb("expert_rec", [P, CHUNKS * SLOTS])
        rank_rec = sb("rank_rec", [P, CHUNKS * SLOTS])
        weight_rec = sb("weight_rec", [P, CHUNKS * SLOTS])

        tiles_f = sb("tiles_f", [P, E])
        tiles_i = sb("tiles_i", [P, E], i32)
        tiles_n = sb("tiles_n", [P, E])
        last_tile = sb("last_tile", [P, E])
        first_slot = sb("first_slot", [P, E])
        past = sb("past", [P, TILE_COLS, E])
        past_tiles = sb("past_tiles", [P, TILE_COLS, E])
        tile_expert = sb("tile_expert", [P, TILE_COLS])
        tile_first = sb("tile_first", [P, TILE_COLS])
        tile_row = sb("tile_row", [P, TILE_COLS])
        tile_row_i = sb("tile_row_i", [P, TILE_COLS], u32)
        expert_row_i = sb("expert_row_i", [1, TILE_COLS * P], i32)

        k_flat = k_diag[:, :, :, :].rearrange("p m t g -> p (m t g)")
        v_flat = v_diag[:, :, :, :].rearrange("p m t g -> p (m t g)")
        x_ring = k_flat[:, 0:4 * 4 * C].rearrange("p (r t f) -> p r t f", r=4, t=4)
        x_ring_t = k_flat[:, 4096:4096 + 4 * C].rearrange("p (t f) -> p t f", t=4)
        base_ring = k_flat[:, 6144:6144 + 2 * BPC * C].rearrange("p (r f) -> p r f", r=2)
        y_ring = v_flat[:, 0:2 * 4 * C].rearrange("p (r f) -> p r f", r=2)
        e_hid = v_flat[:, 2048:2048 + BANK]
        e_hid_t = v_flat[:, 2560:2560 + BANK]
        take_ring = v_flat[:, 4096:4096 + 2 * SLOTS * C].rearrange("p (r s f) -> p r s f", r=2, s=SLOTS)
        at_prob_t = [0]

        def in_prob_t(width):
            at_prob_t[0] += width
            assert at_prob_t[0] <= 4 * BANK
            return prob_t[:, at_prob_t[0] - width:at_prob_t[0]]

        slot_rows = in_prob_t(TILE_COLS * P).bitcast(u32).rearrange("p (g s) -> p g s", s=P)
        slot_rows_f = in_prob_t(TILE_COLS * P).rearrange("p (g s) -> p g s", s=P)
        tile_rows = in_prob_t(TILE_COLS * P).bitcast(u32)
        tile_rows_ring = in_prob_t(4 * 4).bitcast(u32).rearrange("p (r t) -> p r t", r=4)
        slot_at_i = in_prob_t(CHUNKS * SLOTS).bitcast(u32)
        take_i = in_prob_t(2 * SLOTS).bitcast(u32).rearrange("p (r s) -> p r s", r=2)
        take_w = in_prob_t(2 * SLOTS).rearrange("p (r s) -> p r s", r=2)
        slot_at = [prob[:, 0, j * CHUNKS * SLOTS:(j + 1) * CHUNKS * SLOTS] for j in range(2)]
        slot_one = [prob[:, 1, j * CHUNKS * SLOTS:(j + 1) * CHUNKS * SLOTS] for j in range(2)]

        A = [bank(f"bank_a{i}") for i in range(3)]
        Z = [bank(f"bank_z{i}") for i in range(2)]
        U = bank("bank_u")
        Y = [bank(f"bank_y{i}") for i in range(2)]

        names = """w_attn w_ffn const_in const_ready eps_ready table_zero zero_ready
            x_in_done ctx_done res_done q_stored kv_stored qk_read v_read normed_stored base_stored
            ln1_step ln1_var ln1_eps ln1_pow xn_ready t1_full xn_t_ready kv_full kv_out q_full q_out
            s_full s_step s_shifted s_exp p_step p_ready o_full o_taken y_full h2_ready h2_full h2_out
            ln2_step ln2_var ln2_eps ln2_pow xn2_ready t2_full t2_out
            g_full g_out route_step hot_ready rank_full rank_step row_step slot_ready scatter_marked gather_marked take_marked scattered0 scattered1 gap_ready gap_exp weight_step
            z_full z_tanh z_used u_full hid_ready acc_full base_ready
            count_full plan_step plan_ready rows_read rows_f_ready rows_full expert_ready tile_rows_ready
            tile_rows_taken gathered0 gathered1 gathered2 gathered3 xt_full xt_out e_full e_tanh e_hid_ready eh_full eh_out ey_full ey_act ey_dve ey_stored0 ey_stored1
            at_step at_ready take_ready base_read0 base_read1 taken0 taken1 sum_step sum_ready out_stored""".split()
        S = {n: sem(n) for n in names}

        def at(per, c, k):
            return c * per + k

        block = ctx.enter_context(nc.Block())

        @block.sync
        def _(sp):
            def chunk(c, first):
                if not first:
                    sp.wait_ge(S["kv_full"], at(4, c, 0))
                sp.dma_start(ctx_sb[:, :, :], ctx_t[c]).then_inc(S["ctx_done"], 16)
                if not first:
                    sp.wait_ge(S["xn_ready"], at(1, c, 0))
                sp.dma_start(x_sb[:, :, :], x_in[c]).then_inc(S["x_in_done"], 16)
                sp.wait_ge(S["kv_out"], at(4, c, 4))
                sp.dma_start(kv_dram[c], kv_sb[:, :, :]).then_inc(S["kv_stored"], 16)
                sp.wait_ge(S["q_out"], at(2, c, 2))
                sp.dma_start(q_dram[c], q_sb[:, :, :]).then_inc(S["q_stored"], 16)
                if first:
                    sp.wait_ge(S["zero_ready"], 4)
                else:
                    sp.wait_ge(S["s_full"], at(4, c, 0))
                sp.wait_ge(S["kv_stored"], at(16, c, 16))
                sp.wait_ge(S["q_stored"], at(16, c, 16))
                kv = kv_dram[c].rearrange("(t n) (i w f) -> t n i w f", t=8, i=BPC, w=2)
                q = q_dram[c].rearrange("(t n) (i f) -> t n i f", t=8, i=BPC)
                for pair in range(4):
                    for t2 in range(2):
                        src = t2 * 4 + pair
                        t = pair * 2 + t2
                        rows = slice(16 * t, 16 * t + 16)
                        sp.dma_start(k_diag[rows, :, t, :],
                                     kv[src, :, :, 0, :].rearrange("n i (d g) -> d (n i) g", d=D)).then_inc(S["qk_read"], 16)
                        sp.dma_start(q_rows[rows, :, 0:H],
                                     q[src].rearrange("n i (d h) -> d (n i) h", d=D)).then_inc(S["qk_read"], 16)
                if not first:
                    sp.wait_ge(S["o_full"], at(4, c, 0))
                kv_t2 = kv_dram[c].rearrange("(t m) (i w f) -> t m i w f", t=2, i=BPC, w=2)
                for i in range(BPC):
                    for t2 in range(2):
                        r = i * 2 + t2
                        sp.dma_start(v_diag[16 * r:16 * r + 16, :, r, :],
                                     kv_t2[t2, :, i, 1, :].rearrange("m (g d) -> g m d", g=H)).then_inc(S["v_read"], 16)

            chunk(0, True)
            with sp.Fori(1, CHUNKS) as c:
                chunk(c, False)

            y_tiles = expert_out.rearrange("(q t p) f -> q p t f", t=4, p=P)

            def store_quad(q, par):
                sp.wait_ge(S["ey_act"], at(1, q, 1))
                sp.wait_ge(S["ey_dve"], at(1, q, 1))
                sp.dma_start(y_tiles[q], y_ring[:, par, :].rearrange("p (t f) -> p t f", t=4)).then_inc(S[f"ey_stored{par}"], 16)

            with sp.Fori(0, QUADS - 1, 2) as q:
                for r in range(2):
                    store_quad(q + r, r)

            def load_base(c, r):
                sp.dma_start(base_ring[:, r, :], base[c]).then_inc(S[f"base_read{r}"], 16)

            def store_out(c, r):
                sp.wait_ge(S["sum_ready"], at(1, c, 1))
                sp.dma_start(out[c], base_ring[:, r, :]).then_inc(S["out_stored"], 16)

            sp.wait_ge(S["base_stored"], 16 * CHUNKS)
            sp.wait_ge(S["xt_full"], 2 * QUADS)
            load_base(0, 0)
            load_base(1, 1)
            with sp.Fori(0, CHUNKS - 3, 2) as c:
                for r in range(2):
                    store_out(c + r, r)
                    sp.wait_ge(S["out_stored"], at(16, c + r, 16))
                    load_base(c + r + 2, r)
            for r in range(2):
                store_out(CHUNKS - 2 + r, r)
            sp.wait_ge(S["out_stored"], 16 * CHUNKS)

        @block.gpsimd
        def _(pool):
            nc.gpsimd.memset(eps[:, :], EPS).then_inc(S["eps_ready"], 1)
            nc.gpsimd.memset(minus_half[:, :], -0.5).then_inc(S["eps_ready"], 1)
            nc.gpsimd.memset(q_rows[:, :, :], 0.0).then_inc(S["zero_ready"], 1)
            nc.gpsimd.memset(hid[:, :, :], 0.0).then_inc(S["zero_ready"], 1)
            nc.gpsimd.memset(v_diag[:, :, :, :], 0.0).then_inc(S["zero_ready"], 1)

            def ln1_power(c):
                pool.wait_ge(S["ln1_var"], at(1, c, 1))
                nc.gpsimd.tensor_tensor(ln1_eps[:, :], ln1_mv[:, :, 1], eps[:, :], ALU.add).then_inc(S["ln1_eps"], 1)
                pool.wait_ge(S["ln1_eps"], at(1, c, 1))
                nc.gpsimd.tensor_tensor(ln1_rstd[:, :], ln1_eps[:, :], minus_half[:, :], ALU.pow).then_inc(S["ln1_pow"], 1)

            def ln2_power(c):
                pool.wait_ge(S["ln2_var"], at(1, c, 1))
                nc.gpsimd.tensor_tensor(ln2_eps[:, :], ln2_mv[:, :, 1], eps[:, :], ALU.add).then_inc(S["ln2_eps"], 1)
                pool.wait_ge(S["ln2_eps"], at(1, c, 1))
                nc.gpsimd.tensor_tensor(ln2_rstd[:, :], ln2_eps[:, :], minus_half[:, :], ALU.pow).then_inc(S["ln2_pow"], 1)

            def waited(mark, of):
                nc.gpsimd.tensor_tensor(pool_mark[:, mark:mark + 1], eps[:, 0:1], eps[:, 0:1], ALU.add).then_inc(S[of], 1)

            def scatter(c, par):
                pool.wait_ge(S["slot_ready"], at(1, c, 1))
                waited(6 + par, "scatter_marked")
                for s in range(SLOTS):
                    pool.indirect_dma_start(table, bass.IndirectOffsetOnAxis(ap=slot_i[:, par, s:s + 1], axis=0),
                                            row_i[:, par, s % BPC:s % BPC + 1], None).then_inc(S[f"scattered{par}"], 16)

            pool.wait_ge(S["eps_ready"], 2)
            ln1_power(0)
            ln1_power(1)
            ln2_power(0)
            ln1_power(2)
            pool.wait_ge(S["table_zero"], 32)

            def body(c, par, ahead):
                scatter(c - 1, 1 - par)
                ln2_power(c)
                if ahead:
                    ln1_power(c + 2)

            body(1, 1, True)
            with pool.Fori(2, CHUNKS - 3, 2) as c:
                body(c, 0, True)
                body(c + 1, 1, True)
            body(CHUNKS - 2, 0, False)
            body(CHUNKS - 1, 1, False)
            scatter(CHUNKS - 1, 1)
            for par in range(2):
                pool.wait_ge(S[f"scattered{par}"], 16 * SLOTS * CHUNKS // 2)
            pool.wait_ge(S["plan_ready"], 1)
            by_tile = table.rearrange("(r s) o -> r (s o)", s=P)
            for g in range(TILE_COLS):
                pool.indirect_dma_start(slot_rows[:, g, :], None, by_tile,
                                        bass.IndirectOffsetOnAxis(ap=tile_row_i[:, g:g + 1], axis=0)).then_inc(S["rows_read"], 16)
            pool.wait_ge(S["normed_stored"], 16 * CHUNKS)
            pool.wait_ge(S["s_full"], 4 * CHUNKS)

            def gather(q, r, reused):
                pool.wait_ge(S["tile_rows_taken"], at(1, q, 1))
                if reused:
                    pool.wait_ge(S["gather_marked"], at(1, q - 4, 1))
                    pool.wait_ge(S["xt_full"], at(2, q - 4, 2))
                waited(r, "gather_marked")
                for t in range(4):
                    pool.indirect_dma_start(x_ring[:, r, t, :], None, normed,
                                            bass.IndirectOffsetOnAxis(ap=tile_rows_ring[:, r, t:t + 1], axis=0)).then_inc(S[f"gathered{r}"], 16)

            for q in range(4):
                gather(q, q, False)
            with pool.Fori(4, QUADS - 3, 4) as q:
                for r in range(4):
                    gather(q + r, r, True)

            for par in range(2):
                pool.wait_ge(S[f"ey_stored{par}"], 8 * QUADS)

            def take(c, r, reused):
                pool.wait_ge(S["take_ready"], at(1, c, 1))
                if reused:
                    pool.wait_ge(S["take_marked"], at(1, c - 1, 0))
                    pool.wait_ge(S["sum_ready"], at(1, c - 1, 0))
                waited(4 + r, "take_marked")
                for s in range(SLOTS):
                    pool.indirect_dma_start(take_ring[:, r, s, :], None, expert_out,
                                            bass.IndirectOffsetOnAxis(ap=take_i[:, r, s:s + 1], axis=0)).then_inc(S[f"taken{r}"], 16)

            take(0, 0, False)
            take(1, 1, False)
            with pool.Fori(2, CHUNKS - 1, 2) as c:
                for r in range(2):
                    take(c + r, r, True)

        @block.scalar
        def _(act):
            for dst, src in ((ident, ident_in), (before_f, before_in), (iota, iota_in), (row_id, row_id_in), (tile_id, tile_id_in)):
                act.dma_start(dst[:], src).then_inc(S["const_in"], 16)
            for dst, src in ((wkv_sb, wkv), (wq_sb, wq), (wp_sb, wp), (bias_sb, bias)):
                act.dma_start(dst[:], src).then_inc(S["w_attn"], 16)
            act.dma_start(res_t[:, :, :], x_res[0]).then_inc(S["res_done"], 16)
            for dst, src in ((wgate_sb, wgate), (wsh_sb, wsh), (wsh_out_sb, wsh_out), (w1_sb, w1), (w2_sb, w2)):
                act.dma_start(dst[:], src).then_inc(S["w_ffn"], 16)
            act.wait_ge(S["zero_ready"], 4)
            act.dma_start(table[0:NO_TILE * P, :].rearrange("(p s) o -> p (s o)", p=P),
                          hid[:, :, :].rearrange("p s t -> p (s t)")[:, 0:NO_TILE].bitcast(u32)).then_inc(S["table_zero"], 16)
            act.dma_start(table[NO_TILE * P:(NO_TILE + 1) * P, :], hid[:, 0, 0:1].bitcast(u32)).then_inc(S["table_zero"], 16)

            def exps(c):
                for u in range(4):
                    act.wait_ge(S["s_shifted"], at(4, c, u + 1))
                    nc.scalar.activation(prob[:, u, :], prob[:, u, :], ACT.Exp).then_inc(S["s_exp"], 1)

            def project_out(c, first):
                for k in range(KT):
                    act.wait_ge(S["t1_full"], at(KT, c, k + 1))
                    nc.scalar.activation(xn_t[:, k, :], A[(2, 0)[k]][:, :], ACT.Copy).then_inc(S["xn_t_ready"], 1)
                if not first:
                    act.wait_ge(S["kv_stored"], at(16, c, 0))
                    act.wait_ge(S["q_stored"], at(16, c, 0))
                for i in range(BPC):
                    act.wait_ge(S["kv_full"], at(4, c, i + 1))
                    nc.scalar.activation(kv_sb[:, i, :], A[(1, 2, 0, 1)[i]][:, :], ACT.Copy).then_inc(S["kv_out"], 1)
                for i in range(2):
                    act.wait_ge(S["q_full"], at(2, c, i + 1))
                    nc.scalar.activation(q_sb[:, 2 * i:2 * i + 2, :].rearrange("p i f -> p (i f)"), A[(2, 0)[i]][:, :],
                                         ACT.Copy, scale=SCALE).then_inc(S["q_out"], 1)

            def gap_exps(c):
                act.wait_ge(S["gap_ready"], at(1, c, 1))
                nc.scalar.activation(gap_e[:, :], gap[:, :], ACT.Exp).then_inc(S["gap_exp"], 1)

            def tanhs(c, steps, first):
                for s in steps:
                    act.wait_ge(S["z_full"], at(SB, c, s + 1))
                    if not (first and s < 2):
                        act.wait_ge(S["hid_ready"], at(SB, c, s - 1))
                    nc.scalar.activation(th[:, s % 2, :], Z[s % 2][:, :], ACT.Tanh, scale=0.5).then_inc(S["z_tanh"], 1)

            def rows_out(c, par, load):
                for j in range(2):
                    if j == 0:
                        act.wait_ge(S["h2_full"], at(2, c, 1))
                    else:
                        act.wait_ge(S["h2_full"], at(2, c, 2))
                    nc.scalar.activation(h2[:, par, 2 * j:2 * j + 2, :].rearrange("p i f -> p (i f)"), A[(2, 0)[j]][:, :],
                                         ACT.Copy).then_inc(S["h2_out"], 1)
                if load:
                    act.dma_start(res_t[:, :, :], x_res[c + 1]).then_inc(S["res_done"], 16)

            def turned_out(c):
                for k in range(KT):
                    act.wait_ge(S["t2_full"], at(KT, c, k + 1))
                    nc.scalar.activation(xn2_t[:, k, :], A[1 + k][:, :], ACT.Copy).then_inc(S["t2_out"], 1)
                act.dma_start(normed.rearrange("(c p i) f -> c p (i f)", p=P, i=BPC)[c],
                              xn2[:, :, :].rearrange("p i f -> p (i f)")).then_inc(S["normed_stored"], 16)

            def store_base(c, par):
                act.wait_ge(S["base_ready"], at(1, c, 1))
                act.dma_start(base[c], h2[:, par, :, :].rearrange("p i f -> p (i f)")).then_inc(S["base_stored"], 16)

            project_out(0, True)
            exps(0)
            project_out(1, False)
            rows_out(0, 0, True)
            turned_out(0)

            def body(c, par, first, ahead):
                exps(c)
                if ahead:
                    project_out(c + 1, False)
                tanhs(c - 1, range(SB - 1), first)
                gap_exps(c - 1)
                tanhs(c - 1, range(SB - 1, SB), first)
                if not first:
                    act.wait_ge(S["base_stored"], at(16, c - 1, 0))
                rows_out(c, par, ahead)
                store_base(c - 1, 1 - par)
                turned_out(c)

            body(1, 1, True, True)
            with act.Fori(2, CHUNKS - 3, 2) as c:
                body(c, 0, False, True)
                body(c + 1, 1, False, True)
            body(CHUNKS - 2, 0, False, True)
            body(CHUNKS - 1, 1, False, False)
            tanhs(CHUNKS - 1, range(SB), False)
            gap_exps(CHUNKS - 1)
            store_base(CHUNKS - 1, 1)

            def tiles_out(q):
                for j in range(2):
                    act.wait_ge(S["xt_full"], at(2, q, j + 1))
                    nc.scalar.activation(x_ring_t[:, 2 * j:2 * j + 2, :].rearrange("p t f -> p (t f)"), A[j][:, :],
                                         ACT.Copy).then_inc(S["xt_out"], 1)

            def expert_tanh(q, par, first):
                act.wait_ge(S["e_full"], at(1, q, 1))
                if not first:
                    act.wait_ge(S["e_hid_ready"], at(1, q - 1, 0))
                nc.scalar.activation(th[:, par, :], Z[par][:, :], ACT.Tanh, scale=0.5).then_inc(S["e_tanh"], 1)

            def expert_y(q, par, first):
                act.wait_ge(S["ey_full"], at(2, q, 1))
                if not first:
                    act.wait_ge(S[f"ey_stored{par}"], at(8, q - par, 0))
                nc.scalar.activation(y_ring[:, par, 0:BANK], Y[0][:, :], ACT.Copy).then_inc(S["ey_act"], 1)

            act.wait_ge(S["o_full"], 4 * CHUNKS)
            act.wait_ge(S["base_stored"], 16 * CHUNKS)

            def quad(q, par, first, no_wait, last):
                expert_tanh(q, par, no_wait)
                if not last:
                    tiles_out(q + 1)
                if not first:
                    expert_y(q - 1, 1 - par, no_wait or (isinstance(q, int) and q == 2))

            tiles_out(0)
            quad(0, 0, True, True, False)
            quad(1, 1, False, True, False)
            quad(2, 0, False, False, False)
            quad(3, 1, False, False, False)
            with act.Fori(4, QUADS - 3, 2) as q:
                quad(q, 0, False, False, False)
                quad(q + 1, 1, False, False, False)
            quad(QUADS - 2, 0, False, False, False)
            quad(QUADS - 1, 1, False, False, True)
            expert_y(QUADS - 1, 1, False)

        @block.vector
        def _(dve):
            nc.vector.memset(k_diag[:, :, :, :], 0.0).then_inc(S["zero_ready"], 1)
            nc.vector.memset(ones[:, :], 1.0).then_inc(S["const_ready"], 1)
            nc.vector.memset(hot_sum[:, :], 0.0).then_inc(S["const_ready"], 1)
            dve.wait_ge(S["const_in"], 16 * 5)
            nc.vector.tensor_copy(before[:, :], before_f[:, :]).then_inc(S["const_ready"], 1)

            def ln1(c, first):
                dve.wait_ge(S["x_in_done"], at(16, c, 16))
                if not first:
                    dve.wait_ge(S["q_stored"], at(16, c, 0))
                for i in range(BPC):
                    st = nc.vector.bn_stats(ln1_stats[:, i, :], x_sb[:, i, :])
                st.then_inc(S["ln1_step"], 1)
                dve.wait_ge(S["ln1_step"], at(1, c, 1))
                nc.vector.memset(turn_mark[:, :], 0.0)
                for i in range(BPC):
                    st = nc.vector.bn_aggr(ln1_mv[:, i, :], ln1_stats[:, i, :])
                st.then_inc(S["ln1_var"], 1)
                dve.wait_ge(S["ln1_pow"], at(1, c, 1))
                for i in range(BPC):
                    st = nc.vector.tensor_scalar(xn[:, i, :], x_sb[:, i, :], ln1_mv[:, i, 0:1], ln1_rstd[:, i:i + 1],
                                                 ALU.subtract, ALU.mult)
                st.then_inc(S["xn_ready"], 1)

            def softmax(c):
                P_STEPS = 9

                def shift(u):
                    dve.wait_ge(S["s_step"], at(4, c, u + 1))
                    sc = A[u % 3][:, :].rearrange("p (t g) -> p t g", g=H)
                    nc.vector.tensor_tensor(prob[:, u, :].rearrange("p (t g) -> p t g", g=H), sc,
                                            row_max[:, u, :].unsqueeze(2).to_broadcast([P, 32, H]),
                                            ALU.subtract).then_inc(S["s_shifted"], 1)

                for u in range(4):
                    if u == 3:
                        shift(1)
                        shift(2)
                    dve.wait_ge(S["s_full"], at(4, c, u + 1))
                    nc.vector.tensor_reduce(row_max[:, u, :], A[u % 3][:, :].rearrange("p (t g) -> p t g", g=H),
                                            AX.X, ALU.max).then_inc(S["s_step"], 1)
                    if u == 1:
                        shift(0)
                shift(3)
                for u in range(4):
                    dve.wait_ge(S["s_exp"], at(4, c, u + 1))
                    nc.vector.tensor_reduce(row_sum[:, u, :], prob[:, u, :].rearrange("p (t g) -> p t g", g=H),
                                            AX.X, ALU.add).then_inc(S["p_step"], 1)
                dve.wait_ge(S["p_step"], at(P_STEPS, c, 4))
                nc.vector.reciprocal(row_inv[:, :, :], row_sum[:, :, :]).then_inc(S["p_step"], 1)
                dve.wait_ge(S["p_step"], at(P_STEPS, c, 5))
                for u in range(4):
                    pr = prob[:, u, :].rearrange("p (t g) -> p t g", g=H)
                    nc.vector.tensor_tensor(pr, pr, row_inv[:, u, :].unsqueeze(2).to_broadcast([P, 32, H]),
                                            ALU.mult).then_inc(S["p_step"], 1)
                for u in range(4):
                    dve.wait_ge(S["p_step"], at(P_STEPS, c, 6 + u))
                    nc.vector.transpose(prob_t[:, u * BANK:(u + 1) * BANK], prob[:, u, :]).then_inc(S["p_ready"], 1)

            def choose(c, first):
                ROUTE = 3
                dve.wait_ge(S["g_full"], at(1, c, 1))
                nc.vector.transpose(logits[:, :, :].rearrange("p b e -> p (b e)"), A[1][:, 0:P]).then_inc(S["g_out"], 1)
                dve.wait_ge(S["g_out"], at(1, c, 1))
                nc.vector.memset(turn_mark[:, :], 0.0)
                for i in range(BPC):
                    st = nc.vector.max(top[:, i, :], logits[:, i, 0:E])
                st.then_inc(S["route_step"], 1)
                dve.wait_ge(S["route_step"], at(ROUTE, c, 1))
                nc.vector.tensor_tensor(gap[:, :], top[:, :, 1], top[:, :, 0], ALU.subtract).then_inc(S["gap_ready"], 1)
                for i in range(BPC):
                    st = nc.vector.max_index(top_i[:, i, :], top[:, i, :], logits[:, i, 0:E])
                st.then_inc(S["route_step"], 1)
                dve.wait_ge(S["route_step"], at(ROUTE, c, 2))
                nc.vector.tensor_copy(top_f[:, :, :], top_i[:, :, 0:TOP].rearrange("p i j -> p j i")).then_inc(S["route_step"], 1)
                dve.wait_ge(S["route_step"], at(ROUTE, c, 3))
                nc.vector.tensor_copy(expert_rec[:, bass.ds(c * SLOTS, SLOTS)], top_f[:, :, :].rearrange("p j i -> p (j i)"))
                nc.vector.tensor_tensor(hot[:, :, :, :].rearrange("p j i e -> p (j i) e"),
                                        iota[:, :].unsqueeze(1).to_broadcast([P, SLOTS, E]),
                                        top_f[:, :, :].rearrange("p j i -> p (j i)").unsqueeze(2).to_broadcast([P, SLOTS, E]),
                                        ALU.is_equal).then_inc(S["hot_ready"], 1)

            def rank(c, par, first):
                RANK = 5
                hot_s = hot[:, :, :, :].rearrange("p j i e -> p (j i) e")
                dve.wait_ge(S["rank_full"], at(1, c, 1))
                nc.vector.tensor_tensor(hot_pos[:, :, :], A[1][:, 0:P].rearrange("p (s e) -> p s e", e=E), hot_s,
                                        ALU.mult).then_inc(S["rank_step"], 1)
                nc.vector.tensor_reduce(hot_new[:, :], hot[:, :, :, :].rearrange("p j i e -> p e (j i)"), AX.X,
                                        ALU.add).then_inc(S["rank_step"], 1)
                dve.wait_ge(S["rank_step"], at(RANK, c, 1))
                ranks = rank_rec[:, bass.ds(c * SLOTS, SLOTS)]
                nc.vector.tensor_reduce(ranks, hot_pos[:, :, :], AX.X, ALU.add).then_inc(S["rank_step"], 1)
                dve.wait_ge(S["rank_step"], at(RANK, c, 2))
                nc.vector.tensor_tensor(hot_sum[:, :], hot_sum[:, :], hot_new[:, :], ALU.add).then_inc(S["rank_step"], 1)
                dve.wait_ge(S["rank_step"], at(RANK, c, 3))
                nc.vector.scalar_tensor_tensor(out=slot_f[:, :], in0=top_f[:, :, :].rearrange("p j i -> p (j i)"), scalar=float(CAP),
                                               in1=ranks, op0=ALU.mult, op1=ALU.add).then_inc(S["rank_step"], 1)
                if not first:
                    dve.wait_ge(S[f"scattered{par}"], at(8 * SLOTS, c - par, 0))
                    dve.wait_ge(S["row_step"], at(1, c, 0))
                nc.vector.tensor_copy(row_i[:, par, :], row_id[:, :])
                dve.wait_ge(S["rank_step"], at(RANK, c, 5))
                nc.vector.tensor_copy(slot_i[:, par, :], slot_f[:, :]).then_inc(S["slot_ready"], 1)
                nc.vector.tensor_scalar(row_id[:, :], row_id[:, :], float(TOK), None, ALU.add).then_inc(S["row_step"], 1)

            def weigh(c):
                WEIGH = 3
                w = weight_rec[:, bass.ds(c * SLOTS, SLOTS)]
                dve.wait_ge(S["gap_exp"], at(1, c, 1))
                nc.vector.tensor_scalar(gap_1[:, :], gap_e[:, :], 2.0, 2.0, ALU.mult, ALU.add).then_inc(S["weight_step"], 1)
                dve.wait_ge(S["weight_step"], at(WEIGH, c, 1))
                nc.vector.reciprocal(half_inv[:, :], gap_1[:, :]).then_inc(S["weight_step"], 1)
                dve.wait_ge(S["weight_step"], at(WEIGH, c, 2))
                nc.vector.tensor_copy(w[:, 0:BPC], half_inv[:, :])
                nc.vector.tensor_tensor(w[:, BPC:2 * BPC], gap_e[:, :], half_inv[:, :], ALU.mult).then_inc(S["weight_step"], 1)

            def shared_act(c, steps, first):
                for s in steps:
                    dve.wait_ge(S["z_tanh"], at(SB, c, s + 1))
                    nc.vector.scalar_tensor_tensor(out=th[:, s % 2, :], in0=th[:, s % 2, :], scalar=1.0,
                                                   in1=Z[s % 2][:, :], op0=ALU.add, op1=ALU.mult).then_inc(S["z_used"], 1)
                    dve.wait_ge(S["z_used"], at(SB, c, s + 1))
                    dve.wait_ge(S["u_full"], at(SB, c, s + 1))
                    if first and s == 0:
                        dve.wait_ge(S["table_zero"], 32)
                    elif s == 0:
                        dve.wait_ge(S["acc_full"], at(2, c, 0))
                    nc.vector.scalar_tensor_tensor(out=hid[:, s, :], in0=th[:, s % 2, :], scalar=0.5,
                                                   in1=U[:, :], op0=ALU.mult, op1=ALU.mult).then_inc(S["hid_ready"], 1)

            def attention_out(c):
                for u in range(4):
                    dve.wait_ge(S["o_full"], at(4, c, u + 1))
                    nc.vector.transpose(o_t[:, u * BANK:(u + 1) * BANK], A[(2, 0, 1, 2)[u]][:, :]).then_inc(S["o_taken"], 1)

            def residual(c):
                dve.wait_ge(S["res_done"], at(16, c, 16))
                for k in range(KT):
                    dve.wait_ge(S["y_full"], at(KT, c, k + 1))
                    nc.vector.scalar_tensor_tensor(out=res_t[:, k, :], in0=A[k][:, :], scalar=bias_sb[:, k:k + 1],
                                                   in1=res_t[:, k, :], op0=ALU.add, op1=ALU.add).then_inc(S["h2_ready"], 1)

            def ln2_moments(c, par):
                for i in range(BPC):
                    if i % 2 == 0:
                        dve.wait_ge(S["h2_out"], at(2, c, i // 2 + 1))
                    st = nc.vector.bn_stats(ln2_stats[:, i, :], h2[:, par, i, :])
                st.then_inc(S["ln2_step"], 1)
                dve.wait_ge(S["ln2_step"], at(1, c, 1))
                nc.vector.memset(turn_mark[:, :], 0.0)
                for i in range(BPC):
                    st = nc.vector.bn_aggr(ln2_mv[:, i, :], ln2_stats[:, i, :])
                st.then_inc(S["ln2_var"], 1)

            def ln2(c, par, first):
                if not first:
                    dve.wait_ge(S["normed_stored"], at(16, c, 0))
                dve.wait_ge(S["ln2_pow"], at(1, c, 1))
                for i in range(BPC):
                    st = nc.vector.tensor_scalar(xn2[:, i, :], h2[:, par, i, :], ln2_mv[:, i, 0:1], ln2_rstd[:, i:i + 1],
                                                 ALU.subtract, ALU.mult)
                st.then_inc(S["xn2_ready"], 1)

            def base_sum(c, par):
                for j in range(2):
                    dve.wait_ge(S["acc_full"], at(2, c, j + 1))
                    rows = h2[:, par, 2 * j:2 * j + 2, :].rearrange("p i f -> p (i f)")
                    st = nc.vector.tensor_tensor(rows, Y[j][:, :], rows, ALU.add)
                st.then_inc(S["base_ready"], 1)

            ln1(0, True)
            ln1(1, False)
            softmax(0)
            attention_out(0)
            residual(0)
            ln2_moments(0, 0)
            ln2(0, 0, True)
            ln1(2, False)

            def body(c, par, first, second, ahead):
                softmax(c)
                choose(c - 1, first)
                rank(c - 1, 1 - par, first or second)
                shared_act(c - 1, range(SB - 1), first)
                weigh(c - 1)
                attention_out(c)
                residual(c)
                shared_act(c - 1, range(SB - 1, SB), first)
                ln2_moments(c, par)
                ln2(c, par, False)
                base_sum(c - 1, 1 - par)
                if ahead:
                    ln1(c + 2, False)

            body(1, 1, True, False, True)
            body(2, 0, False, True, True)
            body(3, 1, False, False, True)
            with dve.Fori(4, CHUNKS - 3, 2) as c:
                body(c, 0, False, False, True)
                body(c + 1, 1, False, False, True)
            body(CHUNKS - 2, 0, False, False, False)
            body(CHUNKS - 1, 1, False, False, False)
            c = CHUNKS - 1
            choose(c, False)
            rank(c, 1, False)
            shared_act(c, range(SB), False)
            weigh(c)
            base_sum(c, 1)

            step = [0]

            def done(ins):
                step[0] += 1
                ins.then_inc(S["plan_step"], 1)
                dve.wait_ge(S["plan_step"], step[0])

            dve.wait_ge(S["count_full"], 1)
            done(nc.vector.tensor_scalar(tiles_f[:, :], A[0][:, 0:E], float(P - 1), None, ALU.add))
            done(nc.vector.tensor_copy(tiles_i[:, :], tiles_f[:, :]))
            done(nc.vector.tensor_single_scalar(tiles_i[:, :], tiles_i[:, :], P.bit_length() - 1, ALU.arith_shift_right))
            done(nc.vector.tensor_copy(tiles_n[:, :], tiles_i[:, :]))
            done(nc.vector.memset(tiles_f[:, :], 1.0))
            done(nc.vector.tensor_tensor_scan(last_tile[:, :], tiles_f[:, :], tiles_n[:, :], 0.0, ALU.mult, ALU.add))
            done(nc.vector.tensor_tensor(first_slot[:, :], last_tile[:, :], tiles_n[:, :], ALU.subtract))
            done(nc.vector.tensor_scalar(first_slot[:, :], first_slot[:, :], float(P), None, ALU.mult))
            ends = last_tile[:, :].unsqueeze(1).to_broadcast([P, TILE_COLS, E])
            done(nc.vector.tensor_tensor(past[:, :, :], ends, tile_id[:, :].unsqueeze(2).to_broadcast([P, TILE_COLS, E]), ALU.is_le))
            done(nc.vector.tensor_tensor(past_tiles[:, :, :], past[:, :, :], ends, ALU.mult))
            done(nc.vector.tensor_reduce(tile_expert[:, :], past[:, :, :], AX.X, ALU.add))
            done(nc.vector.tensor_reduce(tile_first[:, :], past_tiles[:, :, :], AX.X, ALU.max))
            done(nc.vector.tensor_tensor(tile_row[:, :], tile_id[:, :], tile_first[:, :], ALU.subtract))
            done(nc.vector.scalar_tensor_tensor(out=tile_row[:, :], in0=tile_expert[:, :], scalar=float(CAP // P), in1=tile_row[:, :],
                                                op0=ALU.mult, op1=ALU.add))
            done(nc.vector.tensor_scalar(tile_row[:, :], tile_row[:, :], float(NO_TILE), None, ALU.min))
            done(nc.vector.tensor_scalar(tile_expert[:, :], tile_expert[:, :], float(E - 1), None, ALU.min))
            nc.vector.tensor_copy(tile_row_i[:, :], tile_row[:, :]).then_inc(S["plan_ready"], 1)
            dve.wait_ge(S["rows_read"], 16 * TILE_COLS)
            nc.vector.tensor_copy(slot_rows_f[:, :, :], slot_rows[:, :, :]).then_inc(S["rows_f_ready"], 1)
            dve.wait_ge(S["rows_full"], 1)
            nc.vector.tensor_copy(tile_rows[:, :], A[1][:, 0:TILE_COLS * P]).then_inc(S["tile_rows_ready"], 1)
            nc.vector.tensor_copy(expert_row_i[:, :], A[2][0:1, 0:TILE_COLS * P]).then_inc(S["expert_ready"], 1)
            dve.wait_ge(S["tile_rows_ready"], 1)

            def rows_of(q, r, reused):
                if reused:
                    dve.wait_ge(S[f"gathered{r}"], at(16, q - r - 4, 64))
                nc.vector.tensor_copy(tile_rows_ring[:, r, :], tile_rows[:, bass.ds(q * 4, 4)]).then_inc(S["tile_rows_taken"], 1)

            def expert_act(q, par, first):
                dve.wait_ge(S["e_tanh"], at(1, q, 1))
                if not first:
                    dve.wait_ge(S["eh_full"], at(1, q, 0))
                nc.vector.scalar_tensor_tensor(out=e_hid, in0=th[:, par, :], scalar=1.0, in1=Z[par][:, :],
                                               op0=ALU.add, op1=ALU.mult).then_inc(S["e_hid_ready"], 1)

            def expert_turn(q, first):
                dve.wait_ge(S["eh_full"], at(1, q, 1))
                if not first:
                    dve.wait_ge(S["ey_full"], at(2, q, 0))
                nc.vector.tensor_copy(e_hid_t, U[:, :]).then_inc(S["eh_out"], 1)

            def expert_y(q, par, first):
                dve.wait_ge(S["ey_full"], at(2, q, 2))
                if not first:
                    dve.wait_ge(S[f"ey_stored{par}"], at(8, q - par, 0))
                nc.vector.tensor_copy(y_ring[:, par, BANK:2 * BANK], Y[1][:, :]).then_inc(S["ey_dve"], 1)

            def quad(q, par, r, first, no_wait, more):
                if more:
                    rows_of(q + 4, r, True)
                expert_act(q, par, first)
                if not first:
                    expert_y(q - 1, 1 - par, no_wait)
                expert_turn(q, first)

            for q in range(4):
                rows_of(q, q, False)
            for q in range(4):
                quad(q, q % 2, q, q == 0, q < 3, True)
            with dve.Fori(4, QUADS - 7, 4) as q:
                for r in range(4):
                    quad(q + r, r % 2, r, False, False, True)
            for q in range(QUADS - 4, QUADS):
                quad(q, q % 2, q % 4, False, False, False)
            expert_y(QUADS - 1, 1, False)

            AT = [0]

            def stepped(ins):
                AT[0] += 1
                ins.then_inc(S["at_step"], 1)
                dve.wait_ge(S["at_step"], AT[0])

            for e in range(E):
                before_e = rank_rec if e == 0 else slot_at[(e - 1) % 2]
                stepped(nc.vector.tensor_scalar(slot_one[e % 2], expert_rec[:, :], float(e), first_slot[:, e:e + 1],
                                                ALU.is_equal, ALU.mult))
                stepped(nc.vector.tensor_tensor(slot_at[e % 2], slot_one[e % 2], before_e[:, :], ALU.add))
            stepped(nc.vector.tensor_copy(slot_at_i[:, :], slot_at[(E - 1) % 2]))

            def take_rows(c, r, reused):
                if reused:
                    dve.wait_ge(S[f"taken{r}"], at(8 * SLOTS, c - r - 2, 16 * SLOTS))
                    dve.wait_ge(S["sum_ready"], at(1, c - 2, 1))
                nc.vector.tensor_copy(take_w[:, r, :], weight_rec[:, bass.ds(c * SLOTS, SLOTS)])
                nc.vector.tensor_copy(take_i[:, r, :], slot_at_i[:, bass.ds(c * SLOTS, SLOTS)]).then_inc(S["take_ready"], 1)

            def combine(c, r):
                half = c - r
                dve.wait_ge(S[f"base_read{r}"], at(8, half, 16))
                dve.wait_ge(S[f"taken{r}"], at(8 * SLOTS, half, 16 * SLOTS))
                dve.wait_ge(S["take_ready"], at(1, c, 1))
                for j in range(TOP):
                    for i in range(BPC):
                        s = j * BPC + i
                        rows = base_ring[:, r, i * C:(i + 1) * C]
                        if j:
                            dve.wait_ge(S["sum_step"], at(BPC, c, i + 1))
                        st = nc.vector.scalar_tensor_tensor(out=rows, in0=take_ring[:, r, s, :], scalar=take_w[:, r, s:s + 1],
                                                            in1=rows, op0=ALU.mult, op1=ALU.add)
                        if not j:
                            st.then_inc(S["sum_step"], 1)
                st.then_inc(S["sum_ready"], 1)

            take_rows(0, 0, False)
            take_rows(1, 1, False)
            with dve.Fori(0, CHUNKS - 3, 2) as c:
                for r in range(2):
                    combine(c + r, r)
                    take_rows(c + r + 2, r, True)
            for r in range(2):
                combine(CHUNKS - 2 + r, r)

        @block.tensor
        def _(pe):
            mm = nc.tensor.matmul

            def scores(c, first):
                pe.wait_ge(S["qk_read"], at(256, c, 256))
                if not first:
                    pe.wait_ge(S["t2_out"], at(KT, c, 0))
                for u in range(4):
                    if u == 3:
                        pe.wait_ge(S["s_shifted"], at(4, c, 1))
                    for n in range(4):
                        for a in range(4):
                            m = (u * 4 + n) * 4 + a
                            last = mm(A[u % 3][32 * a:32 * a + 32, n * P:(n + 1) * P], q_rows[:, m, :],
                                      k_diag[:, m, :, :].rearrange("p t g -> p (t g)"), start=True, stop=True)
                    last.then_inc(S["s_full"], 1)

            def gate(c, wait_scores):
                if wait_scores:
                    pe.wait_ge(S["s_shifted"], at(4, c + 1, 2))
                for a in range(4):
                    for k in range(KT):
                        last = mm(A[1][32 * a:32 * a + 32, 0:P], wgate_sb[:, k, :],
                                  xn2_t[:, k, :].rearrange("p (i a t) -> p a i t", a=4, t=32)[:, a],
                                  start=k == 0, stop=k == KT - 1)
                last.then_inc(S["g_full"], 1)

            def project(c, first, gated):
                pe.wait_ge(S["xn_ready"], at(1, c, 1))
                for k in range(KT):
                    if not first:
                        pe.wait_ge(S["s_shifted"], at(4, c - 1, 3 + k))
                    for i in range(BPC):
                        last = nc.tensor.transpose(A[(2, 0)[k]][:, i * P:(i + 1) * P], xn[:, i, k * P:(k + 1) * P], ident[:, :])
                    last.then_inc(S["t1_full"], 1)
                pe.wait_ge(S["ctx_done"], at(16, c, 16))
                for i in range(BPC):
                    if i == 0 and gated:
                        pe.wait_ge(S["g_out"], at(1, c - 1, 0))
                    elif i == 0 and not first:
                        pe.wait_ge(S["s_shifted"], at(4, c - 1, 2))
                    if i in (1, 2):
                        pe.wait_ge(S["xn_t_ready"], at(KT, c, i))
                    if i == 3:
                        pe.wait_ge(S["kv_out"], at(4, c, 1))
                    for k in range(KT):
                        last = mm(A[(1, 2, 0, 1)[i]][:, :], ctx_sb[:, k, i * P:(i + 1) * P], wkv_sb[:, k, :],
                                  start=k == 0, stop=k == KT - 1)
                    last.then_inc(S["kv_full"], 1)
                for i in range(2):
                    pe.wait_ge(S["kv_out"], at(4, c, 2 + i))
                    for j in range(2):
                        t = 2 * i + j
                        for k in range(KT):
                            last = mm(A[(2, 0)[i]][:, j * C:(j + 1) * C], xn_t[:, k, t * P:(t + 1) * P], wq_sb[:, k, :],
                                      start=k == 0, stop=k == KT - 1)
                    last.then_inc(S["q_full"], 1)

            def ranks(c, first, ahead):
                if ahead:
                    pe.wait_ge(S["kv_out"], at(4, c + 2, 4))
                pe.wait_ge(S["hot_ready"], at(1, c, 1))
                if not first:
                    pe.wait_ge(S["rank_step"], at(5, c, 0))
                cols = hot[:, :, :, :].rearrange("p j i e -> p (j i) e")
                mm(A[1][:, 0:P], before[:, :], cols.rearrange("p s e -> p (s e)"), start=True, stop=False)
                for s in range(SLOTS - 1):
                    mm(A[1][:, (s + 1) * E:P], ones[:, :], cols[:, s:s + 1, :].to_broadcast([P, SLOTS - 1 - s, E]), start=False, stop=False,
                       skip_group_check=True)
                mm(A[1][:, 0:P], ones[:, :], hot_sum[:, :].unsqueeze(1).to_broadcast([P, SLOTS, E]), start=False, stop=True).then_inc(S["rank_full"], 1)

            def shared_up(c, steps, first):
                for s in steps:
                    if not (first and s < 2):
                        pe.wait_ge(S["z_used"], at(SB, c, s - 1))
                    for k in range(KT):
                        last = mm(Z[s % 2][:, :], wsh_sb[:, k, s * HID:(s + 1) * HID], xn2_t[:, k, :], start=k == 0, stop=k == KT - 1)
                    last.then_inc(S["z_full"], 1)
                    if not (first and s < 1):
                        pe.wait_ge(S["hid_ready"], at(SB, c, s))
                    for k in range(KT):
                        last = mm(U[:, :], wsh_sb[:, k, SH + s * HID:SH + (s + 1) * HID], xn2_t[:, k, :], start=k == 0, stop=k == KT - 1)
                    last.then_inc(S["u_full"], 1)

            def shared_down(c, first):
                pe.wait_ge(S["hid_ready"], at(SB, c, SB))
                if not first:
                    pe.wait_ge(S["base_ready"], at(1, c, 0))
                for i in range(BPC):
                    for s in range(SB):
                        last = mm(Y[i // 2][:, i % 2 * C:(i % 2 + 1) * C], hid[:, s, i * P:(i + 1) * P], wsh_out_sb[:, s, :],
                                  start=s == 0, stop=s == SB - 1)
                    if i % 2:
                        last.then_inc(S["acc_full"], 1)

            def attend(c, behind, ranked):
                pe.wait_ge(S["v_read"], at(128, c, 128))
                for u in range(4):
                    pe.wait_ge(S["p_ready"], at(4, c, u + 1))
                    if u == 3:
                        pe.wait_ge(S["o_taken"], at(4, c, 1))
                    elif u == 2:
                        if ranked:
                            pe.wait_ge(S["rank_step"], at(5, c - 1, 1))
                        elif behind:
                            pe.wait_ge(S["kv_out"], at(4, c + 1, 4))
                    elif behind:
                        pe.wait_ge(S["q_out"], at(2, c + 1, u + 1))
                    for n in range(4):
                        for pair in range(4):
                            g = (u * 4 + n) * 4 + pair
                            last = mm(A[(2, 0, 1, 2)[u]][32 * pair:32 * pair + 32, n * P:(n + 1) * P],
                                      prob_t[:, 32 * g:32 * g + 32],
                                      v_diag[:, pair * 16 + u * 4 + n, :, :].rearrange("p t d -> p (t d)"), start=True, stop=True)
                    last.then_inc(S["o_full"], 1)
                pe.wait_ge(S["o_taken"], at(4, c, 4))
                cols = o_t.rearrange("p (j n i h) -> p j i n h", j=2, n=8, i=BPC)
                for k in range(KT):
                    for j in range(2):
                        last = mm(A[k][:, :], wp_sb[:, j, k * P:(k + 1) * P], cols[:, j, :, :, 0:H], start=j == 0, stop=j == 1)
                    last.then_inc(S["y_full"], 1)

            def back(c):
                pe.wait_ge(S["h2_ready"], at(KT, c, KT))
                for i in range(BPC):
                    for k in range(KT):
                        last = nc.tensor.transpose(A[(2, 0)[i // 2]][:, i % 2 * C + k * P:i % 2 * C + (k + 1) * P],
                                                   res_t[:, k, i * P:(i + 1) * P], ident[:, :])
                    if i % 2:
                        last.then_inc(S["h2_full"], 1)

            def turn(c):
                pe.wait_ge(S["xn2_ready"], at(1, c, 1))
                pe.wait_ge(S["h2_out"], at(2, c, 2))
                for k in range(KT):
                    for i in range(BPC):
                        last = nc.tensor.transpose(A[1 + k][:, i * P:(i + 1) * P], xn2[:, i, k * P:(k + 1) * P], ident[:, :])
                    last.then_inc(S["t2_full"], 1)

            pe.wait_ge(S["w_attn"], 16 * 4)
            pe.wait_ge(S["const_in"], 16 * 5)
            project(0, True, False)
            scores(0, True)
            project(1, False, False)
            attend(0, True, False)
            pe.wait_ge(S["w_ffn"], 16 * 5)
            pe.wait_ge(S["const_ready"], 3)
            back(0)
            turn(0)

            def body(c, first, ahead):
                scores(c, False)
                gate(c - 1, True)
                if ahead:
                    project(c + 1, False, True)
                ranks(c - 1, first, ahead)
                shared_up(c - 1, range(SB - 1), first)
                attend(c, ahead, True)
                shared_up(c - 1, range(SB - 1, SB), first)
                back(c)
                shared_down(c - 1, first)
                turn(c)

            body(1, True, True)
            with pe.Fori(2, CHUNKS - 1) as c:
                body(c, False, True)
            body(CHUNKS - 1, False, False)
            c = CHUNKS - 1
            pe.wait_ge(S["t2_out"], KT * CHUNKS)
            gate(c, False)
            pe.wait_ge(S["g_out"], CHUNKS)
            ranks(c, False, False)
            shared_up(c, range(SB), False)
            shared_down(c, False)

            pe.wait_ge(S["rank_step"], 5 * CHUNKS)
            mm(A[0][:, 0:E], ones[:, :], hot_sum[:, :], start=True, stop=True).then_inc(S["count_full"], 1)
            pe.wait_ge(S["plan_ready"], 1)
            for g in range(TILE_COLS):
                mm(A[2][0:1, g * P:(g + 1) * P], tile_expert[:, g:g + 1], ident[:, :], start=True, stop=True)
            pe.wait_ge(S["rows_f_ready"], 1)
            for g in range(TILE_COLS):
                last = nc.tensor.transpose(A[1][:, g * P:(g + 1) * P], slot_rows_f[:, g, :], ident[:, :])
            last.then_inc(S["rows_full"], 1)
            pe.wait_ge(S["expert_ready"], 1)

            def tiles_in(q, r, first):
                pe.wait_ge(S[f"gathered{r}"], at(16, q - r, 64))
                for t in range(4):
                    if t % 2 == 0 and not first:
                        pe.wait_ge(S["xt_out"], at(2, q - 1, t // 2 + 1))
                    for k in range(KT):
                        last = nc.tensor.transpose(A[t // 2][:, t % 2 * C + k * P:t % 2 * C + (k + 1) * P],
                                                   x_ring[:, r, t, k * P:(k + 1) * P], ident[:, :])
                    if t % 2:
                        last.then_inc(S["xt_full"], 1)

            def expert_up(q, par, experts, first):
                pe.wait_ge(S["xt_out"], at(2, q, 2))
                if not first:
                    pe.wait_ge(S["e_hid_ready"], at(1, q - 1, 0))
                for t in range(4):
                    for k in range(KT):
                        last = mm(Z[par][:, t * HID:(t + 1) * HID], x_ring_t[:, t, k * P:(k + 1) * P],
                                  w1_sb[:, k, bass.ds(experts[t] * HID, HID)], start=k == 0, stop=k == KT - 1)
                last.then_inc(S["e_full"], 1)

            def expert_turn(q, first):
                pe.wait_ge(S["e_hid_ready"], at(1, q, 1))
                if not first:
                    pe.wait_ge(S["eh_out"], at(1, q, 0))
                for t in range(4):
                    last = nc.tensor.transpose(U[:, t * HID:(t + 1) * HID], e_hid[:, t * HID:(t + 1) * HID], ident[:, :])
                last.then_inc(S["eh_full"], 1)

            def expert_down(q, experts, first):
                pe.wait_ge(S["eh_out"], at(1, q, 1))
                if not first:
                    pe.wait_ge(S["ey_act"], at(1, q, 0))
                    pe.wait_ge(S["ey_dve"], at(1, q, 0))
                for t in range(4):
                    last = mm(Y[t // 2][:, t % 2 * C:(t % 2 + 1) * C], e_hid_t[:, t * HID:(t + 1) * HID],
                              w2_sb[:, bass.ds(experts[t] * C, C)], start=True, stop=True)
                    if t % 2:
                        last.then_inc(S["ey_full"], 1)

            def experts_of(q):
                return [pe.value_load(expert_row_i[0:1, bass.ds(q * 4 + t, 1)], min_val=0, max_val=E - 1) for t in range(4)]

            def quad(q, r, first, second, last):
                expert_up(q, r % 2, experts_of(q), first or second)
                if not last:
                    tiles_in(q + 1, (r + 1) % 4, False)
                if not first:
                    expert_down(q - 1, experts_of(q - 1), second)
                expert_turn(q, first)

            tiles_in(0, 0, True)
            for q in range(4):
                quad(q, q, q == 0, q == 1, False)
            with pe.Fori(4, QUADS - 7, 4) as q:
                for r in range(4):
                    quad(q + r, r, False, False, False)
            for q in range(QUADS - 4, QUADS):
                quad(q, q % 4, False, False, q == QUADS - 1)
            expert_down(QUADS - 1, experts_of(QUADS - 1), False)


def kernel(**inputs):
    import numpy as np
    import concourse.bacc as bacc
    from concourse import mybir as mb
    from concourse.bass_utils import run_bass_kernel_spmd

    a = {k: np.asarray(v) for k, v in inputs.items()}
    x, c_in = a["x"], a["ctx_1024"]
    x7 = x.reshape(CHUNKS, BPC, 8, 2, 4, 2, C)
    c7 = c_in.reshape(CHUNKS, BPC, 8, 2, 4, 2, KT, P)
    heads = lambda w: w.T.reshape(C, H, D)
    by_k = lambda w: w.reshape(KT, P, -1).transpose(1, 0, 2)
    wq = heads(a["L0_xattn_Wq"]).transpose(0, 2, 1).reshape(C, C)
    wk = heads(a["L0_xattn_Wk"]).transpose(0, 2, 1).reshape(C, C)
    wv = a["L0_xattn_Wv"].T
    gate = np.zeros((C, 32), np.float32)
    gate[:, :E] = a["L0_ffn_gate_w"].T
    p = np.arange(P)
    arrays = {
        "x_in": x7.transpose(0, 5, 4, 3, 2, 1, 6).reshape(CHUNKS, P, BPC, C),
        "x_res": x.reshape(CHUNKS, BPC, H, 8, KT, P).transpose(0, 5, 4, 1, 3, 2).reshape(CHUNKS, P, KT, TOK),
        "ctx_t": c7.transpose(0, 7, 6, 1, 5, 4, 3, 2).reshape(CHUNKS, P, KT, TOK),
        "wq": by_k(wq),
        "wkv": by_k(np.concatenate([wk, wv], axis=1)),
        "wp": by_k(a["L0_xattn_Wp"].T),
        "bias": a["L0_xattn_bp"].reshape(KT, P).T,
        "wgate": by_k(gate),
        "wsh": by_k(np.concatenate([a["L0_ffn_sfc1"].T, a["L0_ffn_sfc2"].T], axis=1)),
        "wsh_out": a["L0_ffn_sfc3"].T.reshape(SB, P, C).transpose(1, 0, 2),
        "w1": by_k(a["L0_ffn_w1"].reshape(E * HID, C).T),
        "w2": a["L0_ffn_w2"].transpose(2, 0, 1).reshape(P, E * C),
        "ident": np.eye(P, dtype=np.float32),
        "before": (p[:, None] < p[None, :]).astype(np.float32),
        "iota": np.broadcast_to(np.arange(E, dtype=np.float32), (P, E)),
        "row_id": (p[:, None] * BPC + np.arange(BPC)).astype(np.float32),
        "tile_id": (p[:, None] + P * np.arange(TILE_COLS)).astype(np.float32),
    }
    nc = bacc.Bacc("TRN2", target_bir_lowering=False, num_devices=1)
    given, args = {}, []
    for name, v in arrays.items():
        given[f"in_{name}"] = np.ascontiguousarray(v)
        args.append(nc.dram_tensor(f"in_{name}", v.shape, mb.dt.float32, kind="ExternalInput").ap())
    args.append(nc.dram_tensor("out_0", (CHUNKS, P, BPC * C), mb.dt.float32, kind="ExternalOutput").ap())
    xattn_ffn_kernel(nc, *args)
    r = run_bass_kernel_spmd(nc, [given], core_ids=[0])
    got = np.asarray(r.results[0]["out_0"]).reshape(CHUNKS, 8, H, BPC, C)
    return np.ascontiguousarray(got.transpose(0, 3, 2, 1, 4)).reshape(B, N, C)
```

```python
import concourse.bass as bass
from concourse import mybir
from contextlib import ExitStack

B, N, C = 128, 128, 256
H, D = 16, 16
E, HID = 16, 128
TOP = 2
SH = 512
P = 128
BPC = 4
TOK = BPC * N
CHUNKS = B // BPC
TOKENS = B * N
KT = C // P
GROUPS = TOK // 8
BANK = 512
SB = SH // HID
SLOTS = TOP * BPC
LISTS = TOP * E
TILES = TOKENS // P + E - 1
QUADS = -(-TILES // 16) * 4
TILE_COLS = -(-QUADS * 4 // P)
ROW = C + 2
PAD = 8
PAIRS = E // 2
REGION = TOKENS + 4 * P
NO_TILE = PAIRS * REGION
FAR = 1 << NO_TILE.bit_length()
SCALE = float(D) ** -0.5
EPS = 1e-5


def xattn_ffn_kernel(nc, x_in, x_t_in, x_res, ctx_t, wq, wkv, wp, bias, wgate, wsh, wsh_out, w1, w2,
                     ident_in, before_in, iota_in, row_id_in, tile_id_in, pad_list_in, pad_row_in, out):
    f32, f32r, bf16 = mybir.dt.float32, mybir.dt.float32r, mybir.dt.bfloat16
    i32, u32 = mybir.dt.int32, mybir.dt.uint32
    ALU, ACT, AX = mybir.AluOpType, mybir.ActivationFunctionType, mybir.AxisListType

    ctx = ExitStack()
    with ctx:
        def sb(name, shape, dt=f32):
            return ctx.enter_context(nc.sbuf_tensor(name, shape, dt))

        def bank(name):
            return ctx.enter_context(nc.psum_tensor(name, [P, BANK], f32))

        def sem(name):
            return ctx.enter_context(nc.semaphore(name))

        q_dram = nc.dram_tensor("q_dram", [CHUNKS, P, BPC * C], f32).ap()
        kv_dram = nc.dram_tensor("kv_dram", [CHUNKS, P, BPC * 2 * C], f32).ap()
        slots = [nc.dram_tensor(f"slots{j}", [NO_TILE + P, ROW], f32).ap() for j in range(TOP)]

        bias_sb = sb("bias_sb", [P, C])
        wgate_sb = sb("wgate_sb", [P, KT, 32])
        w2_hi, w2_lo = sb("w2_hi", [P, E * C], f32r), sb("w2_lo", [P, E * C], f32r)

        def weight(where, at, width):
            return where[:, at:at + KT * width].rearrange("p (k f) -> p k f", k=KT)

        wp_hi, wp_lo = weight(w2_hi, 0, C), weight(w2_hi, KT * C, C)
        wq_hi, wq_lo = weight(w2_hi, 2 * KT * C, C), weight(w2_hi, 3 * KT * C, C)
        wkv_hi, wkv_lo = weight(w2_hi, 4 * KT * C, 2 * C), weight(w2_hi, 6 * KT * C, 2 * C)
        wsh_hi, wsh_lo = weight(w2_lo, 0, 2 * SH), weight(w2_lo, KT * 2 * SH, 2 * SH)
        wsh_out_hi, wsh_out_lo = sb("wsh_out_hi", [P, SB, C], f32r), sb("wsh_out_lo", [P, SB, C], f32r)
        ident = sb("ident", [P, P])
        before = sb("before", [P, P], bf16)
        ones = sb("ones", [P, P], bf16)
        iota = sb("iota", [P, E])
        row_id = sb("row_id", [P, BPC])
        tile_id = sb("tile_id", [P, TILE_COLS])
        pad_list = sb("pad_list", [P, E])
        pad_row = sb("pad_row", [P, 6])
        eps = sb("eps", [P, BPC])
        minus_half = sb("minus_half", [P, BPC])
        turn_mark = sb("turn_mark", [P, 1])

        x_sb = sb("x_sb", [P, BPC, C])
        ctx_sb = sb("ctx_sb", [P, KT, TOK])
        q_sb = sb("q_sb", [P, BPC, C])
        w2_sb = sb("w2_sb", [P, E * C])
        kv_sb = w2_sb[:, 0:BPC * 2 * C].rearrange("p (i f) -> p i f", i=BPC)
        q_rows = w2_sb[:, BPC * 2 * C:].rearrange("p (m h) -> p m h", h=32)
        k_diag = sb("k_diag", [P, GROUPS, 8, H])
        v_diag = sb("v_diag", [P, GROUPS, 8, D])
        w1_sb = sb("w1_sb", [P, E * KT * HID])
        prob = w1_sb[:, 0:4 * BANK].rearrange("p (u f) -> p u f", u=4)
        o_t = prob[:, :, :].rearrange("p u f -> p (u f)")
        prob_t = w1_sb[:, 4 * BANK:8 * BANK]
        before_f = prob_t[:, 0:P]
        ones_f = prob_t[:, P:2 * P]
        row_max = sb("row_max", [P, 4, 32])
        row_sum = row_max
        row_inv = sb("row_inv", [P, 4, 32])
        h2 = sb("h2", [P, 2, BPC, C])
        xn2 = sb("xn2", [P, BPC, C + 4])
        row_of = [xn2[:, :, 0:ROW], xn2[:, :, 2:2 + ROW]]
        XN2 = slice(2, 2 + C)
        NUMBER, WEIGHT = (1, C), (0, C + 1)
        CHANNEL = (2, 0)
        ln1_stats = sb("ln1_stats", [P, BPC, 6])
        ln1_mv = sb("ln1_mv", [P, BPC, 2])
        ln1_eps = sb("ln1_eps", [P, BPC])
        ln1_rstd = sb("ln1_rstd", [P, BPC])
        ln2_stats = sb("ln2_stats", [P, BPC, 6])
        ln2_mv = sb("ln2_mv", [P, BPC, 2])
        ln2_eps = sb("ln2_eps", [P, BPC])
        ln2_rstd = sb("ln2_rstd", [P, BPC])
        th = sb("th", [P, 2, TOK])
        hid = sb("hid", [P, 2, TOK])
        hid_hi, hid_lo = sb("hid_hi", [P, SB, TOK], f32r), sb("hid_lo", [P, SB, TOK], f32r)
        x_t, x_hi, x_lo = hid, hid_hi[:, 0:KT, :], hid_lo[:, 0:KT, :]
        ctx_hi, ctx_lo = sb("ctx_hi", [P, KT, TOK], f32r), sb("ctx_lo", [P, KT, TOK], f32r)
        o_hi, o_lo = ctx_hi, ctx_lo
        xn2_t = th
        xn2_hi, xn2_lo = sb("xn2_hi", [P, KT, TOK], f32r), sb("xn2_lo", [P, KT, TOK], f32r)
        wkv_sb = th[:, :, :]
        wq_sb = h2[:, 0, 0:KT, :]
        wp_sb = h2[:, 0, KT:2 * KT, :]
        wsh_out_sb = h2[:, 1, :, :]
        wsh_sb = prob.rearrange("p u f -> p (u f)").rearrange("p (k f) -> p k f", k=KT)

        logits = sb("logits", [P, BPC, 32])
        top = sb("top", [P, BPC, 8])
        top_i = sb("top_i", [P, BPC, 8], u32)
        top_f = sb("top_f", [P, TOP, BPC])
        hot = sb("hot", [P, TOP, BPC, E], bf16)
        hot_new = sb("hot_new", [P, TOP, E])
        hot_sum = sb("hot_sum", [P, TOP, E], bf16)
        hot_pos = logits[:, :, :].rearrange("p b (j e) -> p (b j) e", e=E)
        ranks = sb("ranks", [P, SLOTS])
        down = sb("down", [P, SLOTS])
        slot_up = sb("slot_up", [P, SLOTS])
        slot_turn = sb("slot_turn", [P, SLOTS])
        slot_back = sb("slot_back", [P, SLOTS])
        slot_i = sb("slot_i", [P, TOP, BPC], u32)
        gap = sb("gap", [P, BPC])
        gap_e = sb("gap_e", [P, BPC])
        gap_1 = sb("gap_1", [P, BPC])

        k_flat = k_diag[:, :, :, :].rearrange("p m t g -> p (m t g)")
        v_flat = v_diag[:, :, :, :].rearrange("p m t g -> p (m t g)")
        plan_at = [4 * 4 * ROW + 4 * C]

        def in_plan(*shape):
            size = 1
            for d in shape:
                size *= d
            plan_at[0] += size
            assert plan_at[0] <= 6144
            flat = k_flat[:, plan_at[0] - size:plan_at[0]]
            if len(shape) == 1:
                return flat
            return flat.rearrange("p (a b) -> p a b", a=shape[0]) if len(shape) == 2 else flat.rearrange("p (a b c) -> p a b c", a=shape[0], b=shape[1])

        counts, tiles_f, tiles_n, last_tile, pad_counts = [in_plan(TOP, E) for _ in range(5)]
        tiles_i = in_plan(TOP, E).bitcast(i32)
        past, past_tiles = [in_plan(TOP, TILE_COLS, E) for _ in range(2)]
        tile_expert, tile_first, tile_down, tile_turn, tile_row = [in_plan(TOP, TILE_COLS) for _ in range(5)]
        pad_count, pad_taken, pad_block_f = [in_plan(TOP) for _ in range(3)]
        pad_block = in_plan(TOP).bitcast(i32)
        pad_at = in_plan(3 * TOP)
        pad_at_i = in_plan(3 * TOP).bitcast(u32)

        x_ring = k_flat[:, 0:4 * 4 * ROW].rearrange("p (r t f) -> p r t f", r=4, t=4)
        x_ring_t = k_flat[:, 4 * 4 * ROW:4 * 4 * ROW + 4 * C].rearrange("p (t f) -> p t f", t=4)
        expert_row = k_flat[0:1, 6144:6144 + TOP * QUADS * 4].bitcast(i32)
        slot_row = k_flat[0:1, 7168:7168 + TOP * QUADS * 4].bitcast(i32)
        y_ring = v_flat[:, 0:4 * 4 * C].rearrange("p (r t f) -> p r t f", r=4, t=4)
        e_hi, e_lo = xn2_hi, xn2_lo
        e_hid = v_flat[:, 4096:4096 + 2 * BANK].rearrange("p (r f) -> p r f", r=2)
        pad = v_flat[:, 5632:5632 + PAD * ROW].rearrange("p (s f) -> p s f", s=PAD)
        tail = sb("tail", [P, 4, 4, 2])

        w1_slot = [x_sb, ctx_sb[:, :, :].rearrange("p k (t f) -> p (k t) f", f=C)]

        A = [bank(f"bank_a{i}") for i in range(3)]
        Z = [bank(f"bank_z{i}") for i in range(2)]
        U = bank("bank_u")
        Y = [bank(f"bank_y{i}") for i in range(2)]
        SCORE_BANKS = (A[0], Y[0], Y[1], A[1])
        GATE_BANK = A[2]
        WQ_SUM_BANK = A[2]
        KV_BANKS = (U, A[0], Y[0], Y[1])
        Q_BANKS = (A[1], U)
        U_BANKS = (U, Y[1], U, U)
        O_BANKS = (A[0], Y[0], Y[1], A[1])
        WP_BANKS = (A[0], A[2])
        XN2T_BANKS = (A[2], A[1])

        def o_part(u):
            return o_t[:, u * BANK:(u + 1) * BANK].rearrange("p (n i h) -> p n i h", n=4, i=BPC)[:, :, :, 0:H]

        def by_batch(t, u):
            return t[:, u // 2, :].rearrange("p (i n h) -> p n i h", i=BPC, h=H)[:, u % 2 * 4:u % 2 * 4 + 4]

        names = """w_q w_kv w_p w_ffn w_experts w_split_step w_attn_split w_ffn_split
            ctx_hi_ready ctx_split x_hi_ready x_split xn2_hi_ready xn2_split hid_hi_ready hid_split const_in const_ready eps_ready zero_ready
            x_in_done ctx_done res_done q_stored kv_stored qk_read v_read base_stored
            ln1_step ln1_var ln1_eps ln1_pow x_t_done ones_ready wq_scaled wq_sums kv_full kv_out q_full q_out
            s_full s_step s_shifted s_exp p_step sum_inverse p_scaled p_ready o_full o_taken o_hi_ready o_split o_split_2 y_full res_biased h2_ready
            ln2_step ln2_var ln2_eps ln2_pow xn2_ready t2_full t2_out
            g_full g_out route_step hot_ready rank_full rank_step row_step slot_step slot_ready scatter_marked scattered0 scattered1
            gap_ready gap_exp weight_step
            z_full z_tanh z_used u_full hid_ready acc_full base_ready
            count_full plan_step pad_ready pad_at_ready no_tile_stored padded0 padded1 plan_ready rows_full rows_ready
            slot_free loaded0 loaded1 loaded2 loaded3 tail_ready xt_full xt_out w2_hi_ready w2_split w2_split_2 w1_copied e_full e_tanh e_hid_ready e_hi_ready e_split
            ey_full ey_act ey_dve add_marked added0 added1 added2 added3""".split()
        S = {n: sem(n) for n in names}

        def at(per, c, k):
            return c * per + k

        def choice(n, j):
            return int(n >= QUADS) if isinstance(n, int) else j

        block = ctx.enter_context(nc.Block())

        @block.sync
        def _(sp):
            def chunk(c, first, last):
                if not last:
                    sp.wait_ge(S["ln1_step"], at(1, c, 1))
                    sp.dma_start(x_sb[:, :, :], x_in[c + 1]).then_inc(S["x_in_done"], 16)
                    sp.wait_ge(S["ctx_split"], at(1, c, 1))
                    sp.dma_start(ctx_sb[:, :, :], ctx_t[c + 1]).then_inc(S["ctx_done"], 16)
                sp.wait_ge(S["kv_out"], at(4, c, 4))
                sp.dma_start(kv_dram[c], kv_sb).then_inc(S["kv_stored"], 16)
                sp.wait_ge(S["q_out"], at(2, c, 2))
                sp.dma_start(q_dram[c], q_sb[:, :, :]).then_inc(S["q_stored"], 16)
                if first:
                    sp.wait_ge(S["zero_ready"], 3)
                else:
                    sp.wait_ge(S["s_full"], at(4, c, 0))
                kv = kv_dram[c].rearrange("(t n) (i w f) -> t n i w f", t=8, i=BPC, w=2)
                q = q_dram[c].rearrange("(t n) (i f) -> t n i f", t=8, i=BPC)
                eighths = [(t2 * 4 + pair, pair * 2 + t2) for pair in range(4) for t2 in range(2)]
                sp.wait_ge(S["kv_stored"], at(16, c, 16))
                for src, t in eighths:
                    rows = slice(16 * t, 16 * t + 16)
                    sp.dma_start(k_diag[rows, :, t, :],
                                 kv[src, :, :, 0, :].rearrange("n i (d g) -> d (n i) g", d=D)).then_inc(S["qk_read"], 16)
                sp.wait_ge(S["q_stored"], at(16, c, 16))
                for src, t in eighths:
                    rows = slice(16 * t, 16 * t + 16)
                    sp.dma_start(q_rows[rows, :, 0:H],
                                 q[src].rearrange("n i (d h) -> d (n i) h", d=D)).then_inc(S["qk_read"], 16)
                if not first:
                    sp.wait_ge(S["o_full"], at(4, c, 0))
                kv_t2 = kv_dram[c].rearrange("(t m) (i w f) -> t m i w f", t=2, i=BPC, w=2)
                for i in range(BPC):
                    for t2 in range(2):
                        r = i * 2 + t2
                        sp.dma_start(v_diag[16 * r:16 * r + 16, :, r, :],
                                     kv_t2[t2, :, i, 1, :].rearrange("m (g d) -> g m d", g=H)).then_inc(S["v_read"], 16)

            sp.dma_start(x_sb[:, :, :], x_in[0]).then_inc(S["x_in_done"], 16)
            sp.dma_start(wq_sb, wq).then_inc(S["w_q"], 16)
            sp.dma_start(ctx_sb[:, :, :], ctx_t[0]).then_inc(S["ctx_done"], 16)
            sp.dma_start(wkv_sb, wkv).then_inc(S["w_kv"], 16)
            sp.dma_start(x_t[:, :, :], x_t_in[0]).then_inc(S["x_t_done"], 16)
            sp.dma_start(wp_sb, wp).then_inc(S["w_p"], 16)
            sp.dma_start(bias_sb[:], bias).then_inc(S["w_p"], 16)
            chunk(0, True, False)
            with sp.Fori(1, CHUNKS - 1) as c:
                chunk(c, False, False)
            chunk(CHUNKS - 1, False, True)

            def load_quad(j, q, r, first, row_regs):
                sp.reg_load(row_regs, slot_row[0:1, bass.ds((q + j * QUADS) * 4, 4)])
                rows = [sp.snap(reg, min_val=0, max_val=NO_TILE) for reg in row_regs]
                if not first:
                    sp.wait_ge(S["tail_ready"], at(1, j * QUADS + q - 4, 1))
                    sp.sem_inc(S["slot_free"], 1)
                for t in range(4):
                    sp.dma_start(x_ring[:, r, t, :], slots[j][bass.ds(rows[t], P), :]).then_inc(S[f"loaded{r}"], 16)

            sp.wait_ge(S["s_full"], 4 * CHUNKS)
            sp.wait_ge(S["kv_stored"], 16 * CHUNKS)
            sp.dma_start(w2_sb[:, :], w2).then_inc(S["w_experts"], 16)
            sp.wait_ge(S["y_full"], KT * CHUNKS)
            sp.dma_start(w1_sb[:, :], w1).then_inc(S["w_experts"], 16)
            sp.wait_ge(S["pad_ready"], 1)
            for j in range(TOP):
                sp.dma_start(slots[j][NO_TILE:NO_TILE + P, :], pad[:, 0, :]).then_inc(S["no_tile_stored"], 16)
            row_regs = [sp.alloc_register(f"tile_row{t}") for t in range(4)]
            sp.wait_ge(S["rows_ready"], 1)
            sp.wait_ge(S["no_tile_stored"], 16 * TOP)
            sp.wait_ge(S["scattered0"], 16 * BPC * CHUNKS)
            sp.wait_ge(S["padded0"], 16 * 3)
            for q in range(4):
                load_quad(0, q, q, True, row_regs)
            with sp.Fori(4, QUADS - 3, 4) as q:
                for r in range(4):
                    load_quad(0, q + r, r, False, row_regs)
            sp.wait_ge(S["scattered1"], 16 * BPC * CHUNKS)
            sp.wait_ge(S["padded1"], 16 * 3)
            with sp.Fori(0, QUADS - 3, 4) as q:
                for r in range(4):
                    load_quad(1, q + r, r, False, row_regs)

        @block.gpsimd
        def _(pool):
            nc.gpsimd.memset(eps[:, :], EPS).then_inc(S["eps_ready"], 1)
            nc.gpsimd.memset(minus_half[:, :], -0.5).then_inc(S["eps_ready"], 1)

            def ln1_power(c, first):
                pool.wait_ge(S["ln1_var"], at(1, c, 1))
                nc.gpsimd.tensor_tensor(ln1_eps[:, :], ln1_mv[:, :, 1], eps[:, :], ALU.add).then_inc(S["ln1_eps"], 1)
                pool.wait_ge(S["ln1_eps"], at(1, c, 1))
                if not first:
                    pool.wait_ge(S["q_out"], at(2, c, 0))
                nc.gpsimd.tensor_tensor(ln1_rstd[:, :], ln1_eps[:, :], minus_half[:, :], ALU.pow).then_inc(S["ln1_pow"], 1)

            def ln2_power(c):
                pool.wait_ge(S["ln2_var"], at(1, c, 1))
                nc.gpsimd.tensor_tensor(ln2_eps[:, :], ln2_mv[:, :, 1], eps[:, :], ALU.add).then_inc(S["ln2_eps"], 1)
                pool.wait_ge(S["ln2_eps"], at(1, c, 1))
                nc.gpsimd.tensor_tensor(ln2_rstd[:, :], ln2_eps[:, :], minus_half[:, :], ALU.pow).then_inc(S["ln2_pow"], 1)

            def scatter(c, choices):
                if choices[0] == 0:
                    pool.wait_ge(S["slot_ready"], at(1, c, 1))
                    pool.sem_inc(S["scatter_marked"], 1)
                for j in choices:
                    for i in range(BPC):
                        pool.indirect_dma_start(slots[j], bass.IndirectOffsetOnAxis(ap=slot_i[:, j, i:i + 1], axis=0),
                                                row_of[j][:, i, :], None).then_inc(S[f"scattered{j}"], 16)

            pool.wait_ge(S["eps_ready"], 2)

            def split(lo, value, hi, done):
                nc.gpsimd.tensor_tensor(lo, value[:, :, :], hi, ALU.subtract).then_inc(S[done], 1)

            def ctx_split(c):
                pool.wait_ge(S["ctx_hi_ready"], at(1, c, 1))
                split(ctx_lo[:, :, :], ctx_sb, ctx_hi[:, :, :], "ctx_split")

            def x_split(c):
                pool.wait_ge(S["x_hi_ready"], at(1, c, 1))
                split(x_lo, x_t, x_hi, "x_split")

            def xn2_split(c):
                pool.wait_ge(S["xn2_hi_ready"], at(1, c, 1))
                split(xn2_lo[:, :, :], xn2_t, xn2_hi[:, :, :], "xn2_split")

            def hid_split(c, steps):
                for s in steps:
                    pool.wait_ge(S["hid_hi_ready"], at(SB, c, s + 1))
                    nc.gpsimd.tensor_tensor(hid_lo[:, s, :], hid[:, s % 2, :], hid_hi[:, s, :], ALU.subtract).then_inc(S["hid_split"], 1)

            def scale_probs(c):
                pool.wait_ge(S["sum_inverse"], at(1, c, 1))
                for u in range(2, 4):
                    pr = prob[:, u, :].rearrange("p (t g) -> p t g", g=H)
                    nc.gpsimd.tensor_tensor(pr, pr, row_inv[:, u, :].unsqueeze(2).to_broadcast([P, 32, H]),
                                            ALU.mult).then_inc(S["p_scaled"], 1)

            def o_split(c):
                for u in range(2):
                    pool.wait_ge(S["o_hi_ready"], at(4, c, u + 1))
                    nc.gpsimd.tensor_tensor(by_batch(o_lo, u), o_part(u), by_batch(o_hi, u), ALU.subtract).then_inc(S["o_split"], 1)

            ln1_power(0, True)
            ctx_split(0)
            x_split(0)
            nc.gpsimd.memset(q_rows, 0.0).then_inc(S["zero_ready"], 1)
            nc.gpsimd.memset(v_diag[:, :, :, :], 0.0).then_inc(S["zero_ready"], 1)
            ctx_split(1)
            x_split(1)
            ln1_power(1, False)
            scale_probs(0)
            o_split(0)
            ln2_power(0)
            ctx_split(2)
            ln1_power(2, False)

            def body(c, ahead, ahead_2):
                xn2_split(c - 1)
                if ahead:
                    x_split(c + 1)
                scale_probs(c)
                scatter(c - 1, (0, 1))
                hid_split(c - 1, range(SB - 1))
                o_split(c)
                hid_split(c - 1, range(SB - 1, SB))
                ln2_power(c)
                if ahead_2:
                    ctx_split(c + 2)
                    ln1_power(c + 2, False)

            with pool.Fori(1, CHUNKS - 2) as c:
                body(c, True, True)
            body(CHUNKS - 2, True, False)
            body(CHUNKS - 1, False, False)

            def pads(j):
                blocks = slots[j].rearrange("(b s) f -> b (s f)", s=PAD)
                for g in range(3):
                    pool.indirect_dma_start(blocks if g else slots[j],
                                            bass.IndirectOffsetOnAxis(ap=pad_at_i[:, j * 3 + g:j * 3 + g + 1], axis=0),
                                            pad[:, :, :].rearrange("p s f -> p (s f)") if g else pad[:, 0, :], None,
                                            bounds_check=(NO_TILE + P) // (PAD if g else 1) - 1, oob_is_err=False).then_inc(S[f"padded{j}"], 16)

            xn2_split(CHUNKS - 1)
            scatter(CHUNKS - 1, (0,))
            hid_split(CHUNKS - 1, range(1))
            pool.wait_ge(S["pad_at_ready"], 1)
            pool.wait_ge(S["pad_ready"], 1)
            pads(0)
            hid_split(CHUNKS - 1, range(1, SB))
            scatter(CHUNKS - 1, (1,))
            pool.wait_ge(S["w2_hi_ready"], 1)
            pool.wait_ge(S["u_full"], SB * CHUNKS)
            half = slice(0, E * C // 2)
            nc.gpsimd.tensor_tensor(w2_lo[:, half], w2_sb[:, half], w2_hi[:, half], ALU.subtract).then_inc(S["w2_split"], 1)
            pads(1)

            def add(j, q, r):
                n = j * QUADS + q
                pool.wait_ge(S["ey_act"], at(1, n, 1))
                pool.wait_ge(S["ey_dve"], at(1, n, 1))
                pool.sem_inc(S["add_marked"], 1)
                for t in range(4):
                    pool.indirect_dma_start(out, bass.IndirectOffsetOnAxis(ap=tail[:, r, t, 1 - j:2 - j].bitcast(u32), axis=0),
                                            y_ring[:, r, t, :], None, bounds_check=TOKENS - 1, oob_is_err=False,
                                            compute_op=ALU.add).then_inc(S[f"added{r}"], 16)

            pool.wait_ge(S["base_stored"], 16 * CHUNKS)
            for q in range(4):
                add(0, q, q)
            with pool.Fori(4, QUADS - 3, 4) as q:
                for r in range(4):
                    add(0, q + r, r)
            for r in range(4):
                pool.wait_ge(S[f"added{r}"], 16 * QUADS)
            with pool.Fori(0, QUADS - 3, 4) as q:
                for r in range(4):
                    add(1, q + r, r)
            for r in range(4):
                pool.wait_ge(S[f"added{r}"], 16 * TOP * QUADS)

        @block.scalar
        def _(act):
            def exps(c, us):
                for u in us:
                    act.wait_ge(S["s_shifted"], at(4, c, u + 1))
                    nc.scalar.activation(prob[:, u, :], prob[:, u, :], ACT.Exp).then_inc(S["s_exp"], 1)

            def load_x_t(c):
                act.dma_start(x_t[:, :, :], x_t_in[c]).then_inc(S["x_t_done"], 16)

            def x_round(c):
                act.wait_ge(S["x_t_done"], at(16, c, 16))
                for k in range(KT):
                    st = nc.scalar.activation(x_hi[:, k, :], x_t[:, k, :], ACT.Copy)
                st.then_inc(S["x_hi_ready"], 1)

            def project_out(c, first):
                if not first:
                    act.wait_ge(S["kv_stored"], at(16, c, 0))
                    act.wait_ge(S["q_stored"], at(16, c, 0))
                for i in range(BPC):
                    act.wait_ge(S["kv_full"], at(4, c, i + 1))
                    nc.scalar.activation(kv_sb[:, i, :], KV_BANKS[i][:, :], ACT.Copy).then_inc(S["kv_out"], 1)
                act.wait_ge(S["ln1_pow"], at(1, c, 1))
                for i in range(2):
                    act.wait_ge(S["q_full"], at(2, c, i + 1))
                    for j in range(2):
                        t = 2 * i + j
                        st = nc.scalar.activation(q_sb[:, t, :], Q_BANKS[i][:, j * C:(j + 1) * C], ACT.Copy, scale=ln1_rstd[:, t:t + 1])
                    st.then_inc(S["q_out"], 1)

            def gap_exps(c):
                act.wait_ge(S["gap_ready"], at(1, c, 1))
                nc.scalar.activation(gap_e[:, :], gap[:, :], ACT.Exp).then_inc(S["gap_exp"], 1)

            def ctx_round(c, sums_of):
                act.wait_ge(S["ctx_done"], at(16, c, 16))
                if sums_of is not None:
                    act.wait_ge(S["y_full"], at(2, sums_of, 2))
                for k in range(KT):
                    st = nc.scalar.activation(ctx_hi[:, k, :], ctx_sb[:, k, :], ACT.Copy)
                st.then_inc(S["ctx_hi_ready"], 1)

            def tanhs(c, steps, first):
                for s in steps:
                    act.wait_ge(S["z_full"], at(SB, c, s + 1))
                    if not (first and s < 2):
                        act.wait_ge(S["hid_ready"], at(SB, c, s - 1))
                    nc.scalar.activation(th[:, s % 2, :], Z[s % 2][:, :], ACT.Tanh, scale=0.5).then_inc(S["z_tanh"], 1)

            def hid_round(c, steps):
                for s in steps:
                    act.wait_ge(S["hid_ready"], at(SB, c, s + 1))
                    nc.scalar.activation(hid_hi[:, s, :], hid[:, s % 2, :], ACT.Copy).then_inc(S["hid_hi_ready"], 1)

            def shared_act(c, first, sums_of):
                tanhs(c, range(2), first)
                hid_round(c, range(1))
                tanhs(c, range(2, 3), first)
                hid_round(c, range(1, 2))
                hid_round(c, range(2, 3))
                if sums_of is not None:
                    o_round(sums_of)
                tanhs(c, range(3, SB), first)
                hid_round(c, range(3, SB))

            def load_res(c, par):
                act.dma_start(h2[:, par, :, :], x_res[c]).then_inc(S["res_done"], 16)

            def o_round(c):
                for u in range(4):
                    act.wait_ge(S["o_taken"], at(4, c, u + 1))
                    nc.scalar.activation(by_batch(o_hi, u), o_part(u), ACT.Copy).then_inc(S["o_hi_ready"], 1)

            def turned_out(c):
                for k in range(KT):
                    act.wait_ge(S["t2_full"], at(KT, c, k + 1))
                    nc.scalar.activation(xn2_t[:, k, :], XN2T_BANKS[k][:, :], ACT.Copy).then_inc(S["t2_out"], 1)
                for k in range(KT):
                    act.wait_ge(S["t2_out"], at(KT, c, k + 1))
                    st = nc.scalar.activation(xn2_hi[:, k, :], xn2_t[:, k, :], ACT.Copy)
                st.then_inc(S["xn2_hi_ready"], 1)

            def store_base(c, par):
                act.wait_ge(S["base_ready"], at(2, c, 2))
                act.dma_start(out.rearrange("(c p i) f -> c p (i f)", p=P, i=BPC)[c],
                              h2[:, par, :, :].rearrange("p i f -> p (i f)")).then_inc(S["base_stored"], 16)

            ctx_round(0, None)
            x_round(0)
            for dst, src in ((ident, ident_in), (before_f, before_in), (iota, iota_in), (row_id, row_id_in), (tile_id, tile_id_in),
                             (pad_list, pad_list_in), (pad_row, pad_row_in)):
                act.dma_start(dst[:], src).then_inc(S["const_in"], 16)
            for dst, src in ((wgate_sb[:], wgate), (wsh_sb, wsh), (wsh_out_sb, wsh_out)):
                act.dma_start(dst, src).then_inc(S["w_ffn"], 16)
            act.wait_ge(S["x_split"], 1)
            load_x_t(1)
            project_out(0, True)
            ctx_round(1, None)
            x_round(1)
            project_out(1, False)
            act.wait_ge(S["x_split"], 2)
            load_x_t(2)
            act.wait_ge(S["w_attn_split"], 3)
            load_res(0, 0)
            exps(0, range(4))
            o_round(0)
            ctx_round(2, 0)
            turned_out(0)

            def body(c, par, first, ahead, ahead_2):
                exps(c, range(2))
                if ahead:
                    x_round(c + 1)
                exps(c, range(2, 4))
                gap_exps(c - 1)
                if ahead:
                    project_out(c + 1, False)
                if first:
                    act.wait_ge(S["w_ffn_split"], 2)
                else:
                    act.wait_ge(S["base_stored"], at(16, c - 1, 0))
                load_res(c, par)
                shared_act(c - 1, first, c)
                if ahead_2:
                    ctx_round(c + 2, c)
                    act.wait_ge(S["hid_split"], at(SB, c - 1, SB))
                    load_x_t(c + 2)
                store_base(c - 1, 1 - par)
                turned_out(c)

            body(1, 1, True, True, True)
            with act.Fori(2, CHUNKS - 3, 2) as c:
                body(c, 0, False, True, True)
                body(c + 1, 1, False, True, True)
            body(CHUNKS - 2, 0, False, True, False)
            body(CHUNKS - 1, 1, False, False, False)
            gap_exps(CHUNKS - 1)
            shared_act(CHUNKS - 1, False, None)
            act.wait_ge(S["w_experts"], 32)
            nc.scalar.activation(w2_hi[:, :], w2_sb[:, :], ACT.Copy).then_inc(S["w2_hi_ready"], 1)
            store_base(CHUNKS - 1, 1)


            def tiles_out(q):
                for j in range(2):
                    act.wait_ge(S["xt_full"], at(2, q, j + 1))
                    nc.scalar.activation(x_ring_t[:, 2 * j:2 * j + 2, :].rearrange("p t f -> p (t f)"), A[j][:, :],
                                         ACT.Copy).then_inc(S["xt_out"], 1)

            def expert_tanh(q, par, first):
                act.wait_ge(S["e_full"], at(1, q, 1))
                if not first:
                    act.wait_ge(S["e_hid_ready"], at(1, q - 1, 0))
                nc.scalar.activation(th[:, par, :], Z[par][:, :], ACT.Tanh, scale=0.5).then_inc(S["e_tanh"], 1)

            def e_round(n, par, first):
                act.wait_ge(S["e_hid_ready"], at(1, n, 1))
                if not first:
                    act.wait_ge(S["ey_full"], at(2, n - 1, 0))
                nc.scalar.activation(e_hi[:, par, :], e_hid[:, par, :], ACT.Copy).then_inc(S["e_hi_ready"], 1)

            def expert_y(n, j, r, first):
                act.wait_ge(S["ey_full"], at(2, n, 1))
                act.wait_ge(S["tail_ready"], at(1, n, 1))
                if not first:
                    act.wait_ge(S[f"added{r}"], at(16, n - r, 0))
                for t in range(2):
                    st = nc.scalar.activation(y_ring[:, r, t, :], Y[0][:, t * C:(t + 1) * C], ACT.Copy, scale=tail[:, r, t, j:j + 1])
                st.then_inc(S["ey_act"], 1)

            def quad(n, j, r, before_this, last):
                expert_tanh(n, r % 2, before_this < 2)
                if not last:
                    tiles_out(n + 1)
                e_round(n, r % 2, before_this < 2)
                if before_this:
                    expert_y(n - 1, choice(n - 1, j), (r - 1) % 4, before_this < 5)

            act.wait_ge(S["o_full"], 4 * CHUNKS)
            tiles_out(0)
            for q in range(8):
                quad(q, 0, q % 4, q, False)
            with act.Fori(8, QUADS - 3, 4) as q:
                for r in range(4):
                    quad(q + r, 0, r, 8, False)
            for q in range(QUADS, QUADS + 4):
                quad(q, 1, q % 4, q, False)
            with act.Fori(QUADS + 4, TOP * QUADS - 7, 4) as q:
                for r in range(4):
                    quad(q + r, 1, r, QUADS + 4, False)
            for q in range(TOP * QUADS - 4, TOP * QUADS):
                quad(q, 1, q % 4, q, q == TOP * QUADS - 1)
            expert_y(TOP * QUADS - 1, 1, (TOP * QUADS - 1) % 4, False)

        @block.vector
        def _(dve):
            nc.vector.memset(ones[:, :], 1.0).then_inc(S["const_ready"], 1)
            nc.vector.memset(hot_sum[:, :], 0.0).then_inc(S["const_ready"], 1)

            def ln1_moments(c, first):
                dve.wait_ge(S["x_in_done"], at(16, c, 16))
                for i in range(BPC):
                    st = nc.vector.bn_stats(ln1_stats[:, i, :], x_sb[:, i, :])
                st.then_inc(S["ln1_step"], 1)
                dve.wait_ge(S["ln1_step"], at(1, c, 1))
                if not first:
                    dve.wait_ge(S["ln1_eps"], at(1, c, 0))
                nc.vector.memset(turn_mark[:, :], 0.0)
                for i in range(BPC):
                    st = nc.vector.bn_aggr(ln1_mv[:, i, :], ln1_stats[:, i, :])
                st.then_inc(S["ln1_var"], 1)

            P_STEPS = 6

            def softmax_shift(c):

                def shift(u):
                    dve.wait_ge(S["s_step"], at(4, c, u + 1))
                    sc = SCORE_BANKS[u][:, :].rearrange("p (t g) -> p t g", g=H)
                    nc.vector.tensor_tensor(prob[:, u, :].rearrange("p (t g) -> p t g", g=H), sc,
                                            row_max[:, u, :].unsqueeze(2).to_broadcast([P, 32, H]),
                                            ALU.subtract).then_inc(S["s_shifted"], 1)

                for u in range(4):
                    if u == 3:
                        shift(1)
                        shift(2)
                    dve.wait_ge(S["s_full"], at(4, c, u + 1))
                    nc.vector.tensor_reduce(row_max[:, u, :], SCORE_BANKS[u][:, :].rearrange("p (t g) -> p t g", g=H),
                                            AX.X, ALU.max).then_inc(S["s_step"], 1)
                    if u == 1:
                        shift(0)
                shift(3)

            def softmax_sums(c):
                for u in range(4):
                    dve.wait_ge(S["s_exp"], at(4, c, u + 1))
                    nc.vector.tensor_reduce(row_sum[:, u, :], prob[:, u, :].rearrange("p (t g) -> p t g", g=H),
                                            AX.X, ALU.add).then_inc(S["p_step"], 1)
                dve.wait_ge(S["p_step"], at(P_STEPS, c, 4))
                nc.vector.reciprocal(row_inv[:, :, :], row_sum[:, :, :]).then_inc(S["sum_inverse"], 1)

            def scale_probs(c):
                dve.wait_ge(S["sum_inverse"], at(1, c, 1))
                for u in range(2):
                    pr = prob[:, u, :].rearrange("p (t g) -> p t g", g=H)
                    nc.vector.tensor_tensor(pr, pr, row_inv[:, u, :].unsqueeze(2).to_broadcast([P, 32, H]),
                                            ALU.mult).then_inc(S["p_step"], 1)
                for u in range(2):
                    dve.wait_ge(S["p_step"], at(P_STEPS, c, 5 + u))
                    nc.vector.transpose(prob_t[:, u * BANK:(u + 1) * BANK], prob[:, u, :]).then_inc(S["p_ready"], 1)

            def turn_probs(c):
                for u in range(2, 4):
                    dve.wait_ge(S["p_scaled"], at(2, c, u - 1))
                    nc.vector.transpose(prob_t[:, u * BANK:(u + 1) * BANK], prob[:, u, :]).then_inc(S["p_ready"], 1)

            def logits_out(c):
                dve.wait_ge(S["g_full"], at(1, c, 1))
                nc.vector.transpose(logits[:, :, :].rearrange("p b e -> p (b e)"), GATE_BANK[:, 0:P]).then_inc(S["g_out"], 1)

            def choose(c):
                ROUTE = 3
                dve.wait_ge(S["g_out"], at(1, c, 1))
                nc.vector.memset(turn_mark[:, :], 0.0)
                for i in range(BPC):
                    st = nc.vector.max(top[:, i, :], logits[:, i, 0:E])
                st.then_inc(S["route_step"], 1)
                dve.wait_ge(S["route_step"], at(ROUTE, c, 1))
                nc.vector.tensor_tensor(gap[:, :], top[:, :, 1], top[:, :, 0], ALU.subtract).then_inc(S["gap_ready"], 1)
                for i in range(BPC):
                    st = nc.vector.max_index(top_i[:, i, :], top[:, i, :], logits[:, i, 0:E])
                st.then_inc(S["route_step"], 1)
                dve.wait_ge(S["route_step"], at(ROUTE, c, 2))
                nc.vector.tensor_copy(top_f[:, :, :], top_i[:, :, 0:TOP].rearrange("p i j -> p j i")).then_inc(S["route_step"], 1)
                dve.wait_ge(S["route_step"], at(ROUTE, c, 3))
                nc.vector.tensor_tensor(hot[:, :, :, :].rearrange("p j i e -> p (j i) e"),
                                        iota[:, :].unsqueeze(1).to_broadcast([P, SLOTS, E]),
                                        top_f[:, :, :].rearrange("p j i -> p (j i)").unsqueeze(2).to_broadcast([P, SLOTS, E]),
                                        ALU.is_equal).then_inc(S["hot_ready"], 1)

            def rank(c):
                RANK = 5
                hot_s = hot[:, :, :, :].rearrange("p j i e -> p (j i) e")
                dve.wait_ge(S["rank_full"], at(1, c, 1))
                nc.vector.tensor_tensor(hot_pos[:, :, :], GATE_BANK[:, 0:P].rearrange("p (s e) -> p s e", e=E), hot_s,
                                        ALU.mult).then_inc(S["rank_step"], 1)
                nc.vector.tensor_reduce(hot_new[:, :, :], hot[:, :, :, :].rearrange("p j i e -> p j e i"), AX.X,
                                        ALU.add).then_inc(S["rank_step"], 1)
                dve.wait_ge(S["rank_step"], at(RANK, c, 1))
                nc.vector.tensor_reduce(ranks[:, :], hot_pos[:, :, :], AX.X,
                                        ALU.add).then_inc(S["rank_step"], 1)
                dve.wait_ge(S["rank_step"], at(RANK, c, 2))
                nc.vector.tensor_tensor(hot_sum[:, :, :], hot_sum[:, :, :], hot_new[:, :, :], ALU.add).then_inc(S["rank_step"], 1)
                dve.wait_ge(S["rank_step"], at(RANK, c, 3))
                chosen = top_f[:, :, :].rearrange("p j i -> p (j i)")
                nc.vector.tensor_scalar(down[:, :], chosen, float(PAIRS), None, ALU.is_ge)
                nc.vector.tensor_scalar(slot_turn[:, :], ranks[:, :], -2.0, -float((PAIRS - 1) * REGION + 1), ALU.mult, ALU.add)
                nc.vector.scalar_tensor_tensor(out=slot_up[:, :], in0=chosen, scalar=float(REGION), in1=ranks[:, :],
                                               op0=ALU.mult, op1=ALU.add).then_inc(S["rank_step"], 1)
                for j in range(TOP):
                    st = nc.vector.tensor_copy(xn2[:, :, (1, 2 + C)[j]].bitcast(u32), row_id[:, :])
                st.then_inc(S["row_step"], 1)
                dve.wait_ge(S["rank_step"], at(RANK, c, 5))
                nc.vector.tensor_tensor(slot_back[:, :], slot_turn[:, :], down[:, :], ALU.mult).then_inc(S["slot_step"], 1)
                dve.wait_ge(S["slot_step"], at(1, c, 1))
                nc.vector.tensor_tensor(slot_i[:, :, :].rearrange("p j i -> p (j i)"), slot_up[:, :], slot_back[:, :], ALU.add)
                dve.wait_ge(S["row_step"], at(2, c, 1))
                nc.vector.tensor_scalar(row_id[:, :], row_id[:, :], float(TOK), None, ALU.add).then_inc(S["row_step"], 1)

            def weigh(c):
                WEIGH = 2
                dve.wait_ge(S["gap_exp"], at(1, c, 1))
                nc.vector.tensor_scalar(gap_1[:, :], gap_e[:, :], 2.0, 2.0, ALU.mult, ALU.add).then_inc(S["weight_step"], 1)
                dve.wait_ge(S["weight_step"], at(WEIGH, c, 1))
                nc.vector.reciprocal(xn2[:, :, 0], gap_1[:, :]).then_inc(S["weight_step"], 1)
                dve.wait_ge(S["row_step"], at(2, c, 2))
                dve.wait_ge(S["weight_step"], at(WEIGH, c, 2))
                nc.vector.tensor_tensor(xn2[:, :, 3 + C], gap_e[:, :], xn2[:, :, 0], ALU.mult).then_inc(S["slot_ready"], 1)

            def shared_z(c, s):
                dve.wait_ge(S["z_tanh"], at(SB, c, s + 1))
                nc.vector.scalar_tensor_tensor(out=th[:, s % 2, :], in0=th[:, s % 2, :], scalar=1.0,
                                               in1=Z[s % 2][:, :], op0=ALU.add, op1=ALU.mult).then_inc(S["z_used"], 1)

            def shared_u(c, s, first):
                dve.wait_ge(S["z_used"], at(SB, c, s + 1))
                dve.wait_ge(S["u_full"], at(SB, c, s + 1))
                if not first and s == 0:
                    dve.wait_ge(S["acc_full"], at(2, c, 0))
                if s >= 2:
                    dve.wait_ge(S["hid_split"], at(SB, c, s - 1))
                nc.vector.scalar_tensor_tensor(out=hid[:, s % 2, :], in0=th[:, s % 2, :], scalar=0.5,
                                               in1=U_BANKS[s][:, :], op0=ALU.mult, op1=ALU.mult).then_inc(S["hid_ready"], 1)

            def shared_act(c, steps, first):
                for s in steps:
                    shared_z(c, s)
                    shared_u(c, s, first)

            def attention_out(c):
                for u in range(4):
                    dve.wait_ge(S["o_full"], at(4, c, u + 1))
                    nc.vector.transpose(o_t[:, u * BANK:(u + 1) * BANK], O_BANKS[u][:, :]).then_inc(S["o_taken"], 1)

            def o_split_2(c):
                for u in range(2, 4):
                    dve.wait_ge(S["o_hi_ready"], at(4, c, u + 1))
                    nc.vector.tensor_tensor(by_batch(o_lo, u), o_part(u), by_batch(o_hi, u), ALU.subtract).then_inc(S["o_split_2"], 1)

            def bias_add(c, par):
                dve.wait_ge(S["res_done"], at(16, c, 16))
                nc.vector.tensor_tensor(h2[:, par, :, :], h2[:, par, :, :], bias_sb[:, :].unsqueeze(1).to_broadcast([P, BPC, C]),
                                        ALU.add).then_inc(S["res_biased"], 1)

            def residual(c, par):
                dve.wait_ge(S["res_biased"], at(1, c, 1))
                for j in range(2):
                    dve.wait_ge(S["y_full"], at(2, c, j + 1))
                    rows = h2[:, par, 2 * j:2 * j + 2, :].rearrange("p i f -> p (i f)")
                    nc.vector.tensor_tensor(rows, WP_BANKS[j][:, :], rows, ALU.add).then_inc(S["h2_ready"], 1)
                    dve.wait_ge(S["h2_ready"], at(2, c, j + 1))
                    for i in (2 * j, 2 * j + 1):
                        st = nc.vector.bn_stats(ln2_stats[:, i, :], h2[:, par, i, :])
                st.then_inc(S["ln2_step"], 1)
                dve.wait_ge(S["ln2_step"], at(1, c, 1))
                nc.vector.memset(turn_mark[:, :], 0.0)
                for i in range(BPC):
                    st = nc.vector.bn_aggr(ln2_mv[:, i, :], ln2_stats[:, i, :])
                st.then_inc(S["ln2_var"], 1)

            def ln2(c, par, first):
                if not first:
                    dve.wait_ge(S["scattered0"], at(16 * BPC, c, 0))
                    dve.wait_ge(S["scattered1"], at(16 * BPC, c, 0))
                dve.wait_ge(S["ln2_pow"], at(1, c, 1))
                for i in range(BPC):
                    st = nc.vector.tensor_scalar(xn2[:, i, XN2], h2[:, par, i, :], ln2_mv[:, i, 0:1], ln2_rstd[:, i:i + 1],
                                                 ALU.subtract, ALU.mult)
                st.then_inc(S["xn2_ready"], 1)

            def base_sum(c, par):
                for j in range(2):
                    dve.wait_ge(S["acc_full"], at(2, c, j + 1))
                    rows = h2[:, par, 2 * j:2 * j + 2, :].rearrange("p i f -> p (i f)")
                    nc.vector.tensor_tensor(rows, Y[j][:, :], rows, ALU.add).then_inc(S["base_ready"], 1)

            def split_weights(parts, done):
                for hi, lo, w in parts:
                    n = next(split_steps)
                    nc.vector.tensor_copy(hi[:, :, :], w).then_inc(S["w_split_step"], 1)
                    dve.wait_ge(S["w_split_step"], n)
                    nc.vector.tensor_tensor(lo[:, :, :], w, hi[:, :, :], ALU.subtract).then_inc(S[done], 1)

            split_steps = iter(range(1, 6))
            ln1_moments(0, True)
            nc.vector.memset(ones_f, 1.0).then_inc(S["ones_ready"], 1)
            dve.wait_ge(S["w_q"], 16)
            nc.vector.tensor_scalar(wq_sb, wq_sb, SCALE, None, ALU.mult).then_inc(S["wq_scaled"], 1)
            dve.wait_ge(S["w_kv"], 16)
            split_weights(((wkv_hi, wkv_lo, wkv_sb),), "w_attn_split")
            dve.wait_ge(S["wq_sums"], 1)
            nc.vector.scalar_tensor_tensor(out=wq_sb, in0=WQ_SUM_BANK[:, 0:C].unsqueeze(1).to_broadcast([P, KT, C]), scalar=-1.0 / C,
                                           in1=wq_sb, op0=ALU.mult, op1=ALU.add).then_inc(S["wq_scaled"], 1)
            dve.wait_ge(S["wq_scaled"], 2)
            dve.wait_ge(S["w_p"], 16 * 2)
            split_weights(((wq_hi, wq_lo, wq_sb), (wp_hi, wp_lo, wp_sb)), "w_attn_split")
            ln1_moments(1, False)
            nc.vector.memset(k_diag[:, :, :, :], 0.0).then_inc(S["zero_ready"], 1)
            dve.wait_ge(S["const_in"], 16 * 7)
            nc.vector.tensor_copy(before[:, :], before_f[:, :]).then_inc(S["const_ready"], 1)
            dve.wait_ge(S["w_ffn"], 16 * 3)
            split_weights(((wsh_hi, wsh_lo, wsh_sb), (wsh_out_hi, wsh_out_lo, wsh_out_sb)), "w_ffn_split")
            softmax_shift(0)
            softmax_sums(0)
            scale_probs(0)
            turn_probs(0)
            attention_out(0)
            o_split_2(0)
            bias_add(0, 0)
            residual(0, 0)
            ln2(0, 0, True)
            ln1_moments(2, False)

            def body(c, par, first, ahead):
                softmax_shift(c)
                logits_out(c - 1)
                choose(c - 1)
                softmax_sums(c)
                rank(c - 1)
                weigh(c - 1)
                scale_probs(c)
                turn_probs(c)
                shared_act(c - 1, range(SB - 2), first)
                bias_add(c, par)
                if ahead:
                    ln1_moments(c + 2, False)
                shared_act(c - 1, range(SB - 2, SB - 1), first)
                attention_out(c)
                o_split_2(c)
                shared_z(c - 1, SB - 1)
                shared_u(c - 1, SB - 1, first)
                residual(c, par)
                ln2(c, par, False)
                base_sum(c - 1, 1 - par)

            body(1, 1, True, True)
            with dve.Fori(2, CHUNKS - 3, 2) as c:
                body(c, 0, False, True)
                body(c + 1, 1, False, True)
            body(CHUNKS - 2, 0, False, False)
            body(CHUNKS - 1, 1, False, False)
            nc.vector.memset(pad, 0.0).then_inc(S["plan_step"], 1)
            dve.wait_ge(S["plan_step"], 1)
            for j in range(TOP):
                st = nc.vector.memset(pad[:, :, NUMBER[j]].bitcast(u32), TOKENS)
            st.then_inc(S["pad_ready"], 1)
            c = CHUNKS - 1
            logits_out(c)
            choose(c)
            rank(c)
            weigh(c)
            shared_act(c, range(2), False)

            step = [1]

            def done(ins):
                step[0] += 1
                ins.then_inc(S["plan_step"], 1)
                dve.wait_ge(S["plan_step"], step[0])

            dve.wait_ge(S["count_full"], 1)
            done(nc.vector.tensor_copy(counts[:, :, :].rearrange("p j e -> p (j e)"), A[0][:, 0:LISTS]))
            done(nc.vector.tensor_tensor(pad_counts[:, :, :], counts[:, :, :],
                                         pad_list[:, :].unsqueeze(1).to_broadcast([P, TOP, E]), ALU.mult))
            done(nc.vector.tensor_reduce(pad_count[:, :], pad_counts[:, :, :], AX.X, ALU.add))
            done(nc.vector.tensor_copy(pad_block[:, :], pad_count[:, :]))
            done(nc.vector.tensor_single_scalar(pad_block[:, :], pad_block[:, :], PAD.bit_length() - 1, ALU.arith_shift_right))
            done(nc.vector.tensor_copy(pad_block_f[:, :], pad_block[:, :]))
            done(nc.vector.scalar_tensor_tensor(out=pad_taken[:, :], in0=pad_block_f[:, :], scalar=-float(PAD), in1=pad_count[:, :],
                                                op0=ALU.mult, op1=ALU.add))
            done(nc.vector.tensor_scalar(pad_taken[:, :], pad_taken[:, :], pad_row[:, 5:6], float(FAR), ALU.is_gt, ALU.mult))
            places = pad_at.rearrange("p (j g) -> p j g", j=TOP)
            nc.vector.scalar_tensor_tensor(out=places[:, :, 1:3], in0=pad_block_f.unsqueeze(2).to_broadcast([P, TOP, 2]), scalar=pad_row[:, 3:4],
                                           in1=pad_row[:, 1:3].unsqueeze(1).to_broadcast([P, TOP, 2]), op0=ALU.mult, op1=ALU.add)
            done(nc.vector.scalar_tensor_tensor(out=places[:, :, 0], in0=pad_block_f, scalar=pad_row[:, 4:5],
                                                in1=pad_row[:, 0:1].to_broadcast([P, TOP]), op0=ALU.mult, op1=ALU.add))
            done(nc.vector.tensor_tensor(places[:, :, 0], places[:, :, 0], pad_taken, ALU.add))
            nc.vector.tensor_copy(pad_at_i[:, :], pad_at[:, :]).then_inc(S["pad_at_ready"], 1)
            shared_act(c, range(2, 3), False)
            done(nc.vector.tensor_scalar(tiles_f[:, :, :], counts[:, :, :], float(P - 1), None, ALU.add))
            done(nc.vector.tensor_copy(tiles_i[:, :, :], tiles_f[:, :, :]))
            done(nc.vector.tensor_single_scalar(tiles_i[:, :, :], tiles_i[:, :, :], P.bit_length() - 1, ALU.arith_shift_right))
            done(nc.vector.tensor_copy(tiles_n[:, :, :], tiles_i[:, :, :]))
            done(nc.vector.memset(tiles_f[:, :, :], 1.0))
            for j in range(TOP):
                done(nc.vector.tensor_tensor_scan(last_tile[:, j, :], tiles_f[:, j, :], tiles_n[:, j, :], 0.0, ALU.mult, ALU.add))
            ends = last_tile.unsqueeze(2).to_broadcast([P, TOP, TILE_COLS, E])
            tile_ids = tile_id[:, :].unsqueeze(1).to_broadcast([P, TOP, TILE_COLS])
            done(nc.vector.tensor_tensor(past, ends, tile_ids.unsqueeze(3).to_broadcast([P, TOP, TILE_COLS, E]), ALU.is_le))
            nc.vector.tensor_reduce(tile_expert, past, AX.X, ALU.add)
            done(nc.vector.tensor_tensor(past_tiles, past, ends, ALU.mult))
            done(nc.vector.tensor_reduce(tile_first, past_tiles, AX.X, ALU.max))
            done(nc.vector.tensor_tensor(tile_row, tile_ids, tile_first, ALU.subtract))
            done(nc.vector.tensor_scalar(tile_down[:, :, :], tile_expert[:, :, :], float(PAIRS), None, ALU.is_ge))
            done(nc.vector.tensor_scalar(tile_turn[:, :, :], tile_row[:, :, :], -2.0 * P, -float((PAIRS - 1) * REGION + P), ALU.mult, ALU.add))
            done(nc.vector.tensor_tensor(tile_turn[:, :, :], tile_turn[:, :, :], tile_down[:, :, :], ALU.mult))
            done(nc.vector.scalar_tensor_tensor(out=tile_turn[:, :, :], in0=tile_row[:, :, :], scalar=float(P), in1=tile_turn[:, :, :],
                                                op0=ALU.mult, op1=ALU.add))
            done(nc.vector.scalar_tensor_tensor(out=tile_row[:, :, :], in0=tile_expert[:, :, :], scalar=float(REGION),
                                                in1=tile_turn[:, :, :], op0=ALU.mult, op1=ALU.add))
            done(nc.vector.tensor_scalar(tile_row[:, :, :], tile_row[:, :, :], float(NO_TILE), None, ALU.min))
            nc.vector.tensor_scalar(tile_expert[:, :, :], tile_expert[:, :, :], float(E - 1), float(C), ALU.min,
                                    ALU.mult).then_inc(S["plan_ready"], 1)
            shared_act(c, range(3, SB), False)
            dve.wait_ge(S["rows_full"], 1)
            for table, columns in ((slot_row, A[1]), (expert_row, A[2])):
                st = nc.vector.tensor_copy(table.rearrange("p (j t) -> p j t", j=TOP),
                                           columns[0:1, 0:TOP * TILE_COLS * P].rearrange("p (j t) -> p j t", j=TOP)[:, :, 0:QUADS * 4])
            st.then_inc(S["rows_ready"], 1)
            w1_regs = [dve.alloc_register(f"w1_expert{t}") for t in range(4)]

            def copy_w1(n, par, first):
                dve.reg_load(w1_regs, expert_row[0:1, bass.ds(n * 4, 4)])
                if not first:
                    dve.wait_ge(S["e_full"], at(1, n - 1, 0))
                for t in range(4):
                    st = nc.vector.tensor_copy(w1_slot[par][:, t, :],
                                               w1_sb[:, bass.ds(dve.snap(w1_regs[t], min_val=0, max_val=(E - 1) * C), C)])
                st.then_inc(S["w1_copied"], 1)

            def e_split(n, par):
                dve.wait_ge(S["e_hi_ready"], at(1, n, 1))
                nc.vector.tensor_tensor(e_lo[:, par, :], e_hid[:, par, :], e_hi[:, par, :], ALU.subtract).then_inc(S["e_split"], 1)

            def expert_act(n, par):
                dve.wait_ge(S["e_tanh"], at(1, n, 1))
                nc.vector.scalar_tensor_tensor(out=e_hid[:, par, :], in0=th[:, par, :], scalar=1.0, in1=Z[par][:, :],
                                               op0=ALU.add, op1=ALU.mult).then_inc(S["e_hid_ready"], 1)

            def tails(n, j, r, first):
                dve.wait_ge(S[f"loaded{r}"], at(16, n - r, 64))
                if not first:
                    dve.wait_ge(S[f"added{r}"], at(16, n - r, 0))
                nc.vector.tensor_copy(tail[:, r, :, :], x_ring[:, r, :, (0, C)[j]:(0, C)[j] + 2]).then_inc(S["tail_ready"], 1)

            def expert_y(n, j, r, first):
                dve.wait_ge(S["ey_full"], at(2, n, 2))
                dve.wait_ge(S["tail_ready"], at(1, n, 1))
                if not first:
                    dve.wait_ge(S[f"added{r}"], at(16, n - r, 0))
                for t in range(2, 4):
                    st = nc.vector.tensor_scalar(y_ring[:, r, t, :], Y[1][:, (t - 2) * C:(t - 1) * C], tail[:, r, t, j:j + 1], None, ALU.mult)
                st.then_inc(S["ey_dve"], 1)

            def quad(n, j, r, before_this, last):
                if not last:
                    copy_w1(n + 1, (r + 1) % 2, before_this < 1)
                expert_act(n, r % 2)
                e_split(n, r % 2)
                if before_this:
                    tails(n - 1, choice(n - 1, j), (r - 1) % 4, before_this < 5)
                    expert_y(n - 1, choice(n - 1, j), (r - 1) % 4, before_this < 5)

            dve.wait_ge(S["rows_ready"], 1)
            dve.wait_ge(S["w_experts"], 32)
            copy_w1(0, 0, True)
            base_sum(CHUNKS - 1, 1)
            dve.wait_ge(S["w2_hi_ready"], 1)
            dve.wait_ge(S["u_full"], SB * CHUNKS)
            half = slice(E * C // 2, E * C)
            nc.vector.tensor_tensor(w2_lo[:, half], w2_sb[:, half], w2_hi[:, half], ALU.subtract).then_inc(S["w2_split_2"], 1)
            for q in range(8):
                quad(q, 0, q % 4, q, False)
            with dve.Fori(8, QUADS - 3, 4) as q:
                for r in range(4):
                    quad(q + r, 0, r, 8, False)
            for q in range(QUADS, QUADS + 4):
                quad(q, 1, q % 4, q, False)
            with dve.Fori(QUADS + 4, TOP * QUADS - 7, 4) as q:
                for r in range(4):
                    quad(q + r, 1, r, QUADS + 4, False)
            for q in range(TOP * QUADS - 4, TOP * QUADS):
                quad(q, 1, q % 4, q, q == TOP * QUADS - 1)
            last = TOP * QUADS - 1
            tails(last, 1, last % 4, False)
            expert_y(last, 1, last % 4, False)

        @block.tensor
        def _(pe):
            mm = nc.tensor.matmul

            def mm_split(out, lhs_hi, lhs_lo, rhs_hi, rhs_lo, start, stop):
                mm(out, lhs_hi, rhs_hi, start=start, stop=False)
                mm(out, lhs_hi, rhs_lo, start=False, stop=False)
                return mm(out, lhs_lo, rhs_hi, start=False, stop=stop)

            def scores(c, first, second):
                pe.wait_ge(S["qk_read"], at(256, c, 256))
                for u in range(4):
                    if first and u < 3:
                        pe.wait_ge(S["kv_out"], at(4, 1, u + 2))
                    elif first:
                        pe.wait_ge(S["q_out"], at(2, 1, 1))
                    elif u in (1, 2) and not second:
                        pe.wait_ge(S["base_ready"], at(2, c - 2, u))
                    elif u == 3:
                        pe.wait_ge(S["t2_out"], at(KT, c - 1, KT))
                    for n in range(4):
                        for a in range(4):
                            m = (u * 4 + n) * 4 + a
                            last = mm(SCORE_BANKS[u][32 * a:32 * a + 32, n * P:(n + 1) * P], q_rows[:, m, :],
                                      k_diag[:, m, :, :].rearrange("p t g -> p (t g)"), start=True, stop=True)
                    last.then_inc(S["s_full"], 1)

            def gate(c):
                pe.wait_ge(S["t2_out"], at(KT, c, KT))
                for a in range(4):
                    for k in range(KT):
                        last = mm(GATE_BANK[32 * a:32 * a + 32, 0:P], wgate_sb[:, k, :],
                                  xn2_t[:, k, :].rearrange("p (i a t) -> p a i t", a=4, t=32)[:, a],
                                  start=k == 0, stop=k == KT - 1)
                last.then_inc(S["g_full"], 1)

            def project(c, first, gated, ranks_first=None):
                if first:
                    pe.wait_ge(S["ones_ready"], 1)
                    pe.wait_ge(S["wq_scaled"], 1)
                    for k in range(KT):
                        last = mm(WQ_SUM_BANK[:, 0:C], ones_f, wq_sb[:, k, :], start=k == 0, stop=k == KT - 1)
                    last.then_inc(S["wq_sums"], 1)
                    pe.wait_ge(S["w_attn_split"], 1)
                pe.wait_ge(S["ctx_split"], at(1, c, 1))
                for i in range(BPC):
                    if gated and i:
                        pe.wait_ge(S["s_shifted"], at(4, c - 1, i))
                    elif not gated and not first and i:
                        pe.wait_ge(S["kv_out"], at(4, c - 1, i + 1))
                    elif not gated and not first:
                        pe.wait_ge(S["q_out"], at(2, c - 1, 2))
                    for k in range(KT):
                        tokens = slice(i * P, (i + 1) * P)
                        last = mm_split(KV_BANKS[i][:, :], ctx_hi[:, k, tokens], ctx_lo[:, k, tokens],
                                        wkv_hi[:, k, :], wkv_lo[:, k, :], k == 0, k == KT - 1)
                    last.then_inc(S["kv_full"], 1)
                if ranks_first is not None:
                    ranks(c - 2, ranks_first)
                if first:
                    pe.wait_ge(S["w_attn_split"], 2)
                pe.wait_ge(S["x_split"], at(1, c, 1))
                for i in range(2):
                    if i == 1:
                        pe.wait_ge(S["kv_out"], at(4, c, 1))
                    elif gated:
                        pe.wait_ge(S["s_shifted"], at(4, c - 1, 4))
                    elif not first:
                        pe.wait_ge(S["q_out"], at(2, c - 1, 1))
                    for j in range(2):
                        t = 2 * i + j
                        tokens = slice(t * P, (t + 1) * P)
                        for k in range(KT):
                            last = mm_split(Q_BANKS[i][:, j * C:(j + 1) * C], x_hi[:, k, tokens], x_lo[:, k, tokens],
                                            wq_hi[:, k, :], wq_lo[:, k, :], k == 0, k == KT - 1)
                    last.then_inc(S["q_full"], 1)

            def ranks(c, first):
                pe.wait_ge(S["hot_ready"], at(1, c, 1))
                if not first:
                    pe.wait_ge(S["rank_step"], at(5, c, 0))
                place = GATE_BANK[:, 0:P].rearrange("p (j i e) -> p j i e", j=TOP, e=E)
                mm(GATE_BANK[:, 0:P], before[:, :], hot[:, :, :, :].rearrange("p j i e -> p (j i e)"), start=True, stop=False)
                for i in range(BPC - 1):
                    mm(place[:, :, i + 1:, :], ones[:, :], hot[:, :, i:i + 1, :].to_broadcast([P, TOP, BPC - 1 - i, E]),
                       start=False, stop=False, skip_group_check=True)
                mm(GATE_BANK[:, 0:P], ones[:, :], hot_sum[:, :, :].unsqueeze(2).to_broadcast([P, TOP, BPC, E]),
                   start=False, stop=True).then_inc(S["rank_full"], 1)

            def shared_z(c, s, first):
                if not (first and s < 2):
                    pe.wait_ge(S["z_used"], at(SB, c, s - 1))
                cols = slice(s * HID, (s + 1) * HID)
                for k in range(KT):
                    last = mm_split(Z[s % 2][:, :], wsh_hi[:, k, cols], wsh_lo[:, k, cols], xn2_hi[:, k, :], xn2_lo[:, k, :],
                                    k == 0, k == KT - 1)
                last.then_inc(S["z_full"], 1)

            def shared_u(c, s, first, ahead):
                if s == 0 and ahead:
                    pe.wait_ge(S["q_out"], at(2, c + 2, 2))
                if s == 0 and not first:
                    pe.wait_ge(S["hid_ready"], at(SB, c, 0))
                elif s >= 2:
                    pe.wait_ge(S["hid_ready"], at(SB, c, (1, 3)[s - 2]))
                cols = slice(SH + s * HID, SH + (s + 1) * HID)
                for k in range(KT):
                    last = mm_split(U_BANKS[s][:, :], wsh_hi[:, k, cols], wsh_lo[:, k, cols], xn2_hi[:, k, :], xn2_lo[:, k, :],
                                    k == 0, k == KT - 1)
                last.then_inc(S["u_full"], 1)

            def shared_in(c, first):
                if first:
                    pe.wait_ge(S["w_ffn_split"], 2)
                pe.wait_ge(S["xn2_split"], at(1, c, 1))

            def shared_down(c, first):
                pe.wait_ge(S["hid_split"], at(SB, c, SB - 1))
                if not first:
                    pe.wait_ge(S["base_ready"], at(2, c, 0))

                def part(i, s):
                    tokens = slice(i * P, (i + 1) * P)
                    return mm_split(Y[i // 2][:, i % 2 * C:(i % 2 + 1) * C], hid_hi[:, s, tokens], hid_lo[:, s, tokens],
                                    wsh_out_hi[:, s, :], wsh_out_lo[:, s, :], s == 0, s == SB - 1)

                for i in (0, 1):
                    for j in (i, i + 2):
                        for s in range(SB - 1):
                            part(j, s)
                    pe.wait_ge(S["hid_split"], at(SB, c, SB))
                    for j in (i, i + 2):
                        last = part(j, SB - 1)
                        if i:
                            last.then_inc(S["acc_full"], 1)

            def attend(c, first, behind):
                pe.wait_ge(S["v_read"], at(128, c, 128))
                for u in range(4):
                    pe.wait_ge(S["p_ready"], at(4, c, u + 1))
                    if behind and u < 3:
                        pe.wait_ge(S["kv_out"], at(4, c + 1, u + 2))
                    elif behind:
                        pe.wait_ge(S["q_out"], at(2, c + 1, 1))
                    if u == 2 and not first:
                        pe.wait_ge(S["hid_ready"], at(SB, c - 1, 2))
                    for n in range(4):
                        for pair in range(4):
                            g = (u * 4 + n) * 4 + pair
                            last = mm(O_BANKS[u][32 * pair:32 * pair + 32, n * P:(n + 1) * P],
                                      prob_t[:, 32 * g:32 * g + 32],
                                      v_diag[:, pair * 16 + u * 4 + n, :, :].rearrange("p t d -> p (t d)"), start=True, stop=True)
                    last.then_inc(S["o_full"], 1)

            def attend_out(c, ranked):
                pe.wait_ge(S["o_split"], at(2, c, 2))
                pe.wait_ge(S["o_split_2"], at(2, c, 2))
                if ranked:
                    pe.wait_ge(S["rank_step"], at(5, c - 1, 1))
                else:
                    pe.wait_ge(S["w_attn_split"], 3)
                for i in range(BPC):
                    for j in range(2):
                        tokens = slice(i * P, (i + 1) * P)
                        last = mm_split(WP_BANKS[i // 2][:, i % 2 * C:(i % 2 + 1) * C], o_hi[:, j, tokens], o_lo[:, j, tokens],
                                        wp_hi[:, j, :], wp_lo[:, j, :], j == 0, j == 1)
                    if i % 2:
                        last.then_inc(S["y_full"], 1)

            def turn(c):
                pe.wait_ge(S["xn2_ready"], at(1, c, 1))
                for k in range(KT):
                    for i in range(BPC):
                        last = nc.tensor.transpose(XN2T_BANKS[k][:, i * P:(i + 1) * P], xn2[:, i, 2 + k * P:2 + (k + 1) * P], ident[:, :])
                    last.then_inc(S["t2_full"], 1)

            project(0, True, False)
            project(1, False, False)
            scores(0, True, False)
            attend(0, True, False)
            attend_out(0, False)
            pe.wait_ge(S["w_ffn"], 16 * 3)
            pe.wait_ge(S["const_in"], 16 * 7)
            pe.wait_ge(S["const_ready"], 3)
            turn(0)

            def body(c, first, ahead):
                scores(c, False, first)
                gate(c - 1)
                if ahead:
                    project(c + 1, False, True, first)
                shared_in(c - 1, first)
                shared_z(c - 1, 0, first)
                if not ahead:
                    ranks(c - 1, False)
                shared_u(c - 1, 0, first, ahead)
                shared_z(c - 1, 1, first)
                if not ahead:
                    pe.wait_ge(S["s_shifted"], at(4, c, 3))
                shared_u(c - 1, 1, first, ahead)
                shared_z(c - 1, 2, first)
                shared_u(c - 1, 2, first, ahead)
                attend(c, False, ahead)
                shared_z(c - 1, SB - 1, first)
                shared_u(c - 1, SB - 1, first, ahead)
                attend_out(c, True)
                shared_down(c - 1, first)
                turn(c)

            body(1, True, True)
            with pe.Fori(2, CHUNKS - 1) as c:
                body(c, False, True)
            body(CHUNKS - 1, False, False)
            c = CHUNKS - 1
            gate(c)
            ranks(c, False)
            shared_in(c, False)
            shared_z(c, 0, False)
            pe.wait_ge(S["rank_step"], 5 * CHUNKS)
            mm(A[0][:, 0:LISTS], ones[:, :], hot_sum[:, :, :].rearrange("p j e -> p (j e)"), start=True, stop=True).then_inc(S["count_full"], 1)
            shared_u(c, 0, False, False)
            pe.wait_ge(S["base_ready"], at(2, c, 0))
            for s in range(1, SB):
                shared_z(c, s, False)
                shared_u(c, s, False, False)
            pe.wait_ge(S["plan_ready"], 1)
            for j in range(TOP):
                for g in range(TILE_COLS):
                    col = (j * TILE_COLS + g) * P
                    mm(A[1][0:1, col:col + P], tile_row[:, j, g:g + 1], ident[:, :], start=True, stop=True)
                    last = mm(A[2][0:1, col:col + P], tile_expert[:, j, g:g + 1], ident[:, :], start=True, stop=True)
            last.then_inc(S["rows_full"], 1)
            shared_down(c, False)
            pe.wait_ge(S["rows_ready"], 1)

            def tiles_in(n, j, r):
                pe.wait_ge(S[f"loaded{r}"], at(16, n - r, 64))
                for t in range(4):
                    for k in range(KT):
                        last = nc.tensor.transpose(A[t // 2][:, t % 2 * C + k * P:t % 2 * C + (k + 1) * P],
                                                   x_ring[:, r, t, CHANNEL[j] + k * P:CHANNEL[j] + (k + 1) * P], ident[:, :])
                    if t % 2:
                        last.then_inc(S["xt_full"], 1)

            expert_regs = [[pe.alloc_register(f"expert{r}_{t}") for t in range(4)] for r in range(4)]

            def load_experts(n, r):
                pe.reg_load(expert_regs[r], expert_row[0:1, bass.ds(n * 4, 4)])

            def expert_cols(r, t):
                return bass.ds(pe.snap(expert_regs[r][t], min_val=0, max_val=(E - 1) * C), C)

            def expert_up(n, r):
                pe.wait_ge(S["w1_copied"], at(1, n, 1))
                pe.wait_ge(S["xt_out"], at(2, n, 2))
                for t in range(4):
                    for k in range(KT):
                        last = mm(Z[r % 2][:, t * P:(t + 1) * P], w1_slot[r % 2][:, t, k * HID:(k + 1) * HID],
                                  x_ring_t[:, t, k * P:(k + 1) * P], start=k == 0, stop=k == KT - 1)
                last.then_inc(S["e_full"], 1)

            def expert_down(n, r, first):
                pe.wait_ge(S["e_split"], at(1, n, 1))
                if first:
                    pe.wait_ge(S["w2_split"], 1)
                    pe.wait_ge(S["w2_split_2"], 1)
                else:
                    pe.wait_ge(S["ey_act"], at(1, n, 0))
                    pe.wait_ge(S["ey_dve"], at(1, n, 0))
                for t in range(4):
                    slots, cols = slice(t * P, (t + 1) * P), expert_cols(r, t)
                    last = mm_split(Y[t // 2][:, t % 2 * C:(t % 2 + 1) * C], e_hi[:, r % 2, slots], e_lo[:, r % 2, slots],
                                    w2_hi[:, cols], w2_lo[:, cols], True, True)
                    if t % 2:
                        last.then_inc(S["ey_full"], 1)

            def quad(n, j, q, r, before_this, last):
                expert_up(n, r)
                if not last:
                    load_experts(n + 1, (r + 1) % 4)
                    tiles_in(n + 1, 1 if isinstance(q, int) and q == QUADS - 1 else j, (r + 1) % 4)
                if before_this:
                    expert_down(n - 1, (r - 1) % 4, before_this < 2)

            pe.wait_ge(S["w_experts"], 32)
            load_experts(0, 0)
            tiles_in(0, 0, 0)
            for q in range(4):
                quad(q, 0, q, q, q, False)
            with pe.Fori(4, QUADS - 7, 4) as q:
                for r in range(4):
                    quad(q + r, 0, q + r, r, 4, False)
            for q in range(QUADS - 4, QUADS):
                quad(q, 0, q, q % 4, 4, False)
            with pe.Fori(0, QUADS - 7, 4) as q:
                for r in range(4):
                    quad(q + r + QUADS, 1, q + r, r, QUADS, False)
            for q in range(QUADS - 4, QUADS):
                quad(QUADS + q, 1, q, q % 4, QUADS, q == QUADS - 1)
            last_quad = TOP * QUADS - 1
            expert_down(last_quad, last_quad % 4, False)


def kernel(**inputs):
    import numpy as np
    import concourse.bacc as bacc
    from concourse import mybir as mb
    from concourse.bass_utils import run_bass_kernel_spmd

    a = {k: np.asarray(v) for k, v in inputs.items()}
    x, c_in = a["x"], a["ctx_1024"]
    x7 = x.reshape(CHUNKS, BPC, 8, 2, 4, 2, C)
    c7 = c_in.reshape(CHUNKS, BPC, 8, 2, 4, 2, KT, P)
    heads = lambda w: w.T.reshape(C, H, D)
    by_k = lambda w: w.reshape(KT, P, -1).transpose(1, 0, 2)
    wq = heads(a["L0_xattn_Wq"]).transpose(0, 2, 1).reshape(C, C)
    wk = heads(a["L0_xattn_Wk"]).transpose(0, 2, 1).reshape(C, C)
    wv = a["L0_xattn_Wv"].T
    gate = np.zeros((C, 32), np.float32)
    gate[:, :E] = a["L0_ffn_gate_w"].T
    p = np.arange(P)
    e, s = p // PAD, p % PAD
    sign = np.where(e < PAIRS, 1, -1)
    start = np.where(e < PAIRS, e * REGION, (e - PAIRS + 1) * REGION - 1)
    block = np.where(e < PAIRS, e * (REGION // PAD), (e - PAIRS + 1) * (REGION // PAD) - 1)
    pad_row = np.stack([start + sign * s, block + sign * (s + 1), block + sign * (s + 1 + PAD),
                        sign, sign * PAD, s], axis=1)
    arrays = {
        "x_in": x7.transpose(0, 5, 4, 3, 2, 1, 6).reshape(CHUNKS, P, BPC, C),
        "x_t_in": x.reshape(CHUNKS, BPC, 8, 2, 4, 2, KT, P).transpose(0, 7, 6, 1, 5, 4, 3, 2).reshape(CHUNKS, P, KT, TOK),
        "x_res": x.reshape(CHUNKS, BPC, H, 8, C).transpose(0, 3, 2, 1, 4).reshape(CHUNKS, P, BPC, C),
        "ctx_t": c7.transpose(0, 7, 6, 1, 5, 4, 3, 2).reshape(CHUNKS, P, KT, TOK),
        "wq": by_k(wq),
        "wkv": by_k(np.concatenate([wk, wv], axis=1)),
        "wp": by_k(a["L0_xattn_Wp"].T),
        "bias": np.broadcast_to(a["L0_xattn_bp"], (P, C)),
        "wgate": by_k(gate),
        "wsh": by_k(np.concatenate([a["L0_ffn_sfc1"].T, a["L0_ffn_sfc2"].T], axis=1)),
        "wsh_out": a["L0_ffn_sfc3"].T.reshape(SB, P, C).transpose(1, 0, 2),
        "w1": a["L0_ffn_w1"].reshape(E, HID, KT, P).transpose(3, 0, 2, 1).reshape(P, E * KT * HID),
        "w2": a["L0_ffn_w2"].transpose(2, 0, 1).reshape(P, E * C),
        "ident": np.eye(P, dtype=np.float32),
        "before": (p[:, None] < p[None, :]).astype(np.float32),
        "iota": np.broadcast_to(np.arange(E, dtype=np.float32), (P, E)),
        "row_id": (p[:, None] * BPC + np.arange(BPC)).astype(np.float32),
        "tile_id": (p[:, None] + P * np.arange(TILE_COLS)).astype(np.float32),
        "pad_list": (p[:, None] // PAD == np.arange(E)).astype(np.float32),
        "pad_row": pad_row.astype(np.float32),
    }
    nc = bacc.Bacc("TRN2", target_bir_lowering=False, num_devices=1)
    given, args = {}, []
    for name, v in arrays.items():
        given[f"in_{name}"] = np.ascontiguousarray(v)
        args.append(nc.dram_tensor(f"in_{name}", v.shape, mb.dt.float32, kind="ExternalInput").ap())
    args.append(nc.dram_tensor("out_0", (TOKENS, C), mb.dt.float32, kind="ExternalOutput").ap())
    xattn_ffn_kernel(nc, *args)
    r = run_bass_kernel_spmd(nc, [given], core_ids=[0])
    got = np.asarray(r.results[0]["out_0"]).reshape(CHUNKS, 8, H, BPC, C)
    return np.ascontiguousarray(got.transpose(0, 3, 2, 1, 4)).reshape(B, N, C)
```
